# Optimizing a Trainium2 kernel written in Bass

```python
import numpy as np
import jax
import jax.numpy as jnp

def _softmax(x, axis=-1):
    return jax.nn.softmax(x, axis=axis)
def _gelu(x):
    return jax.nn.gelu(x, approximate=True)
def _silu(x):
    return jax.nn.silu(x)
def _sigmoid(x):
    return jax.nn.sigmoid(x)
def _layernorm(x, axis=-1, eps=1e-5):
    m = jnp.mean(x, axis=axis, keepdims=True)
    v = jnp.var(x, axis=axis, keepdims=True)
    return (x - m) / jnp.sqrt(v + eps)
def _scatter_add(tgt, idx, src, axis=0):
    return tgt.at[idx].add(src)
def _segment_sum(src, seg, n):
    return jax.ops.segment_sum(src, seg, n)

kernel_name = 'mk_conv_preact_d4_conv_nchw256_3a5a90'

def setup_inputs(seed: int = 0):
    np.random.seed(seed)
    _w = jnp.asarray
    def _rec_inputs():
        import jax
        import jax.numpy as jnp
        _gk = jax.random.key(seed)
        x = -0.0009896 + 1 * jax.random.normal(jax.random.fold_in(_gk, 1), (2, 256, 56, 56), jnp.float32)
        return x
    x = _rec_inputs()
    def _L0_conv_setup():
        import jax, jax.numpy as jnp
        import numpy as np
        WS = 7

        def _attn_idx(H, W, ws):
            Ho, Wo = (H - (ws - 1), W - (ws - 1))
            idx = np.arange(Ho * Wo, dtype=np.int64).reshape(Ho, Wo)
            pad = ws // 2
            idx = np.pad(idx, pad, mode='edge')
            return jnp.asarray(idx.reshape(-1))

        def _bias_idx(H, W, ws):
            rep_h = np.ones(ws, dtype=np.int64)
            rep_h[ws // 2] = H - (ws - 1)
            rep_w = np.ones(ws, dtype=np.int64)
            rep_w[ws // 2] = W - (ws - 1)
            idx_h = np.repeat(np.arange(ws), rep_h)
            idx_w = np.repeat(np.arange(ws), rep_w)
            bias_hw = idx_h[:, None] * (2 * ws - 1) + idx_w[None, :]
            idx_k = (np.arange(ws)[:, None] * (2 * ws - 1) + np.arange(ws)).reshape(-1)
            bias_idx = bias_hw.reshape(-1)[:, None] + idx_k[None, :]
            return jnp.asarray(bias_idx)
        key = jax.random.key(seed)
        k0, k1, k2, k3 = jax.random.split(key, 4)
        B, C, H, W = (2, 256, 56, 56)
        nh = 8
        x = jax.random.normal(k0, (B, C, H, W), jnp.float32)
        qkv_w = jax.random.normal(k1, (3 * C, C), jnp.float32) * 0.02
        qkv_b = jnp.zeros((3 * C,), jnp.float32)
        proj_w = jax.random.normal(k2, (C, C), jnp.float32) * 0.02
        proj_b = jnp.zeros((C,), jnp.float32)
        relative_bias = jax.random.normal(k3, ((2 * WS - 1) ** 2, nh), jnp.float32) * 0.02
        return {'x': x, 'qkv_w': qkv_w, 'qkv_b': qkv_b, 'proj_w': proj_w, 'proj_b': proj_b, 'relative_bias': relative_bias}
    _L0_conv_all = _L0_conv_setup()
    _L0_conv_in = {k: v for k, v in _L0_conv_all.items() if k in ('qkv_w', 'qkv_b', 'proj_w', 'proj_b', 'relative_bias', )}
    del _L0_conv_all

    def _L1_conv_setup():
        import jax, jax.numpy as jnp
        import numpy as np
        PAD0, PAD1 = (2, 1)
        UPSAMPLE_FACTOR = 2

        def _make_kernel():
            k = jnp.array([1.0, 3.0, 3.0, 1.0], dtype=jnp.float32)
            k2 = k[None, :] * k[:, None]
            k2 = k2 / jnp.sum(k2)
            return k2 * UPSAMPLE_FACTOR ** 2
        key = jax.random.key(seed)
        x = jax.random.normal(key, (8, 256, 256, 256), dtype=jnp.float32)
        kernel = _make_kernel()
        return {'x': x, 'kernel': kernel}
    _L1_conv_all = _L1_conv_setup()
    _L1_conv_in = {k: v for k, v in _L1_conv_all.items() if k in ('kernel', )}
    del _L1_conv_all

    def _L2_conv_setup():
        import jax, jax.numpy as jnp
        import numpy as np
        C = 256
        EPS = 1e-05
        key = jax.random.key(seed)
        ks = jax.random.split(key, 10)
        N, H, W = (4, 64, 64)
        Ch = C // 2
        sc = 1.0 / np.sqrt(C)
        sch = 1.0 / np.sqrt(Ch)
        return {'x': jax.random.normal(ks[0], (N, C, H, W), dtype=jnp.float32), 'cfc': jax.random.normal(ks[1], (C, 2), dtype=jnp.float32) * 0.1, 'theta_w': jax.random.normal(ks[2], (Ch, C), dtype=jnp.float32) * sc, 'theta_b': jax.random.normal(ks[3], (Ch,), dtype=jnp.float32) * 0.01, 'phi_w': jax.random.normal(ks[4], (Ch, C), dtype=jnp.float32) * sc, 'phi_b': jax.random.normal(ks[5], (Ch,), dtype=jnp.float32) * 0.01, 'g_w': jax.random.normal(ks[6], (Ch, C), dtype=jnp.float32) * sc, 'g_b': jax.random.normal(ks[7], (Ch,), dtype=jnp.float32) * 0.01, 'out_w': jax.random.normal(ks[8], (C, Ch), dtype=jnp.float32) * sch, 'out_b': jax.random.normal(ks[9], (C,), dtype=jnp.float32) * 0.01}
    _L2_conv_all = _L2_conv_setup()
    _L2_conv_in = {k: v for k, v in _L2_conv_all.items() if k in ('cfc', 'theta_w', 'theta_b', 'phi_w', 'phi_b', 'g_w', 'g_b', 'out_w', 'out_b', )}
    del _L2_conv_all

    def _L3_conv_setup():
        import jax, jax.numpy as jnp
        import numpy as np
        import math
        HEADS = 4
        DIM_HEAD = 32
        CH = 256
        GRID_SIZE = 5
        SPLINE_ORDER = 3
        GRID_LO, GRID_HI = (-6.0, 6.0)
        N_COEF = GRID_SIZE + SPLINE_ORDER
        _h = (GRID_HI - GRID_LO) / GRID_SIZE
        GRID = jnp.asarray(np.arange(-SPLINE_ORDER, GRID_SIZE + SPLINE_ORDER + 1) * _h + GRID_LO, dtype=jnp.float32)

        def b_splines(x):
            xe = x[..., None]
            bases = ((xe >= GRID[:-1]) & (xe < GRID[1:])).astype(x.dtype)
            for k in range(1, SPLINE_ORDER + 1):
                left = (xe - GRID[:-(k + 1)]) / (GRID[k:-1] - GRID[:-(k + 1)]) * bases[..., :-1]
                right = (GRID[k + 1:] - xe) / (GRID[k + 1:] - GRID[1:-k]) * bases[..., 1:]
                bases = left + right
            return bases

        def _safe(x, lo=-6.0, hi=6.0):
            return jnp.clip(jnp.nan_to_num(x, nan=0.0, posinf=hi, neginf=lo), lo, hi)
        key = jax.random.key(seed)
        ks = jax.random.split(key, 8)
        inner = HEADS * DIM_HEAD
        B, H, W = (2, 32, 32)
        s = 1.0 / math.sqrt(CH)
        x = jax.random.normal(ks[0], (B, CH, H, W), dtype=jnp.float32)
        Wq = jax.random.normal(ks[1], (inner, CH), dtype=jnp.float32) * s
        Wk = jax.random.normal(ks[2], (inner, CH), dtype=jnp.float32) * s
        Wv = jax.random.normal(ks[3], (inner, CH), dtype=jnp.float32) * s
        Wo = jax.random.normal(ks[4], (CH, inner), dtype=jnp.float32) * (1.0 / math.sqrt(inner))
        base_w = jax.random.normal(ks[5], (1, 1), dtype=jnp.float32)
        spline_w = jax.random.normal(ks[6], (1, 1, N_COEF), dtype=jnp.float32) * 0.1
        spline_scaler = jnp.ones((1, 1), dtype=jnp.float32)
        return {'x': x, 'Wq': Wq, 'Wk': Wk, 'Wv': Wv, 'Wo': Wo, 'base_w': base_w, 'spline_w': spline_w, 'spline_scaler': spline_scaler}
    _L3_conv_all = _L3_conv_setup()
    _L3_conv_in = {k: v for k, v in _L3_conv_all.items() if k in ('Wq', 'Wk', 'Wv', 'Wo', 'base_w', 'spline_w', 'spline_scaler', )}
    del _L3_conv_all

    return {
        "x": x,
        "L0_conv_qkv_w": _L0_conv_in["qkv_w"],
        "L0_conv_qkv_b": _L0_conv_in["qkv_b"],
        "L0_conv_proj_w": _L0_conv_in["proj_w"],
        "L0_conv_proj_b": _L0_conv_in["proj_b"],
        "L0_conv_relative_bias": _L0_conv_in["relative_bias"],
        "L1_conv_kernel": _L1_conv_in["kernel"],
        "L2_conv_cfc": _L2_conv_in["cfc"],
        "L2_conv_theta_w": _L2_conv_in["theta_w"],
        "L2_conv_theta_b": _L2_conv_in["theta_b"],
        "L2_conv_phi_w": _L2_conv_in["phi_w"],
        "L2_conv_phi_b": _L2_conv_in["phi_b"],
        "L2_conv_g_w": _L2_conv_in["g_w"],
        "L2_conv_g_b": _L2_conv_in["g_b"],
        "L2_conv_out_w": _L2_conv_in["out_w"],
        "L2_conv_out_b": _L2_conv_in["out_b"],
        "L3_conv_Wq": _L3_conv_in["Wq"],
        "L3_conv_Wk": _L3_conv_in["Wk"],
        "L3_conv_Wv": _L3_conv_in["Wv"],
        "L3_conv_Wo": _L3_conv_in["Wo"],
        "L3_conv_base_w": _L3_conv_in["base_w"],
        "L3_conv_spline_w": _L3_conv_in["spline_w"],
        "L3_conv_spline_scaler": _L3_conv_in["spline_scaler"],
    }

def reference(x, L0_conv_qkv_w, L0_conv_qkv_b, L0_conv_proj_w, L0_conv_proj_b, L0_conv_relative_bias, L1_conv_kernel, L2_conv_cfc, L2_conv_theta_w, L2_conv_theta_b, L2_conv_phi_w, L2_conv_phi_b, L2_conv_g_w, L2_conv_g_b, L2_conv_out_w, L2_conv_out_b, L3_conv_Wq, L3_conv_Wk, L3_conv_Wv, L3_conv_Wo, L3_conv_base_w, L3_conv_spline_w, L3_conv_spline_scaler):
    import jax
    import jax.numpy as jnp
    def _L0_conv_ref(x, qkv_w, qkv_b, proj_w, proj_b, relative_bias):
        import jax, jax.numpy as jnp
        import numpy as np
        WS = 7

        def _attn_idx(H, W, ws):
            Ho, Wo = (H - (ws - 1), W - (ws - 1))
            idx = np.arange(Ho * Wo, dtype=np.int64).reshape(Ho, Wo)
            pad = ws // 2
            idx = np.pad(idx, pad, mode='edge')
            return jnp.asarray(idx.reshape(-1))

        def _bias_idx(H, W, ws):
            rep_h = np.ones(ws, dtype=np.int64)
            rep_h[ws // 2] = H - (ws - 1)
            rep_w = np.ones(ws, dtype=np.int64)
            rep_w[ws // 2] = W - (ws - 1)
            idx_h = np.repeat(np.arange(ws), rep_h)
            idx_w = np.repeat(np.arange(ws), rep_w)
            bias_hw = idx_h[:, None] * (2 * ws - 1) + idx_w[None, :]
            idx_k = (np.arange(ws)[:, None] * (2 * ws - 1) + np.arange(ws)).reshape(-1)
            bias_idx = bias_hw.reshape(-1)[:, None] + idx_k[None, :]
            return jnp.asarray(bias_idx)
        B, C, H, W = x.shape
        ws = WS
        nh = relative_bias.shape[1]
        hd = C // nh
        scale = hd ** (-0.5)
        L = (H - ws + 1) * (W - ws + 1)
        qkv = jnp.einsum('oc,bchw->bohw', qkv_w, x) + qkv_b[None, :, None, None]
        q, k, v = (qkv[:, :C], qkv[:, C:2 * C], qkv[:, 2 * C:])
        q = q * scale

        def unfold(t):
            p = jax.lax.conv_general_dilated_patches(t, (ws, ws), (1, 1), 'VALID')
            return p.reshape(B, C, L, ws * ws)
        attn_idx = _attn_idx(H, W, ws)
        bias_idx = _bias_idx(H, W, ws)
        k_u = unfold(k).reshape(B, nh, hd, L, ws * ws).transpose(0, 1, 3, 2, 4)
        v_u = unfold(v).reshape(B, nh, hd, L, ws * ws).transpose(0, 1, 3, 4, 2)
        k_g = k_u[:, :, attn_idx]
        v_g = v_u[:, :, attn_idx]
        qh = q.reshape(B, nh, hd, H * W).transpose(0, 1, 3, 2)
        attn = jnp.einsum('bnld,bnldk->bnlk', qh, k_g)
        bias = jnp.transpose(relative_bias[bias_idx], (2, 0, 1))
        attn = attn + bias[None]
        out = jnp.einsum('bnlk,bnlkd->bnld', attn, v_g)
        out = jnp.transpose(out, (0, 1, 3, 2)).reshape(B, C, H, W)
        out = jnp.einsum('oc,bchw->bohw', proj_w, out) + proj_b[None, :, None, None]
        return out

    def _L1_conv_ref(x, kernel):
        import jax, jax.numpy as jnp
        import numpy as np
        PAD0, PAD1 = (2, 1)
        UPSAMPLE_FACTOR = 2

        def _make_kernel():
            k = jnp.array([1.0, 3.0, 3.0, 1.0], dtype=jnp.float32)
            k2 = k[None, :] * k[:, None]
            k2 = k2 / jnp.sum(k2)
            return k2 * UPSAMPLE_FACTOR ** 2
        N, C, H, W = x.shape
        kh, kw = kernel.shape
        xp = jnp.pad(x, ((0, 0), (0, 0), (PAD0, PAD1), (PAD0, PAD1)))
        k = jnp.flip(kernel)[None, None, :, :]
        xr = xp.reshape(N * C, 1, H + PAD0 + PAD1, W + PAD0 + PAD1)
        out = jax.lax.conv_general_dilated(xr, k, window_strides=(1, 1), padding='VALID', dimension_numbers=('NCHW', 'OIHW', 'NCHW'))
        Ho = H + PAD0 + PAD1 - kh + 1
        Wo = W + PAD0 + PAD1 - kw + 1
        return out.reshape(N, C, Ho, Wo)

    def _L2_conv_ref(x, cfc, theta_w, theta_b, phi_w, phi_b, g_w, g_b, out_w, out_b):
        import jax, jax.numpy as jnp
        import numpy as np
        C = 256
        EPS = 1e-05
        N, Cc, H, W = x.shape
        L = H * W
        xf = x.reshape(N, Cc, L)
        mean = jnp.mean(xf, axis=2)
        var = jnp.var(xf, axis=2, ddof=1) + EPS
        std = jnp.sqrt(var)
        z = mean * cfc[None, :, 0] + std * cfc[None, :, 1]
        gate = jax.nn.sigmoid(z)[:, :, None]
        s = xf * gate
        theta = jnp.einsum('oc,ncl->nol', theta_w, s) + theta_b[None, :, None]
        phi = jnp.einsum('oc,ncl->nol', phi_w, s) + phi_b[None, :, None]
        g = jnp.einsum('oc,ncl->nol', g_w, s) + g_b[None, :, None]
        attn = jax.nn.softmax(jnp.einsum('nci,ncj->nij', theta, phi), axis=-1)
        nl = jnp.einsum('ncj,nij->nci', g, attn)
        nl = jnp.einsum('oc,ncl->nol', out_w, nl) + out_b[None, :, None]
        out = s + nl
        return out.reshape(N, Cc, H, W)

    def _L3_conv_ref(x, Wq, Wk, Wv, Wo, base_w, spline_w, spline_scaler):
        import jax, jax.numpy as jnp
        import numpy as np
        import math
        HEADS = 4
        DIM_HEAD = 32
        CH = 256
        GRID_SIZE = 5
        SPLINE_ORDER = 3
        GRID_LO, GRID_HI = (-6.0, 6.0)
        N_COEF = GRID_SIZE + SPLINE_ORDER
        _h = (GRID_HI - GRID_LO) / GRID_SIZE
        GRID = jnp.asarray(np.arange(-SPLINE_ORDER, GRID_SIZE + SPLINE_ORDER + 1) * _h + GRID_LO, dtype=jnp.float32)

        def b_splines(x):
            xe = x[..., None]
            bases = ((xe >= GRID[:-1]) & (xe < GRID[1:])).astype(x.dtype)
            for k in range(1, SPLINE_ORDER + 1):
                left = (xe - GRID[:-(k + 1)]) / (GRID[k:-1] - GRID[:-(k + 1)]) * bases[..., :-1]
                right = (GRID[k + 1:] - xe) / (GRID[k + 1:] - GRID[1:-k]) * bases[..., 1:]
                bases = left + right
            return bases

        def _safe(x, lo=-6.0, hi=6.0):
            return jnp.clip(jnp.nan_to_num(x, nan=0.0, posinf=hi, neginf=lo), lo, hi)
        B, C, H, W = x.shape
        N = H * W
        h, dh = (HEADS, DIM_HEAD)

        def proj(Wp):
            return jnp.einsum('bchw,ic->bihw', x, Wp).reshape(B, h, dh, N)
        q = proj(Wq).transpose(0, 1, 3, 2)
        k = proj(Wk)
        v = proj(Wv).transpose(0, 1, 3, 2)
        sim = jnp.einsum('bhnd,bhdm->bhnm', q, k) / math.sqrt(dh)
        xs = _safe(sim)
        coef = (spline_w * spline_scaler[..., None])[0, 0]
        kan = base_w[0, 0] * jax.nn.silu(xs) + jnp.einsum('...k,k->...', b_splines(xs), coef)
        attn = jax.nn.softmax(kan, axis=-1)
        out = jnp.einsum('bhnm,bhmd->bhnd', attn, v)
        out = out.transpose(0, 1, 3, 2).reshape(B, h * dh, H, W)
        return jnp.einsum('bihw,ci->bchw', out, Wo)

    def _gn(v, G=32, eps=1e-5):
        B_, C_, H_, W_ = v.shape
        g = v.reshape(B_, G, C_ // G, H_, W_)
        m = jnp.mean(g, axis=(2, 3, 4), keepdims=True)
        s = jnp.var(g, axis=(2, 3, 4), keepdims=True)
        return ((g - m) / jnp.sqrt(s + eps)).reshape(v.shape)

    def _ln_c(v, eps=1e-6):
        m = jnp.mean(v, axis=1, keepdims=True)
        s = jnp.var(v, axis=1, keepdims=True)
        return (v - m) / jnp.sqrt(s + eps)

    def _ln_t(v, eps=1e-5):
        m = jnp.mean(v, axis=-1, keepdims=True)
        s = jnp.var(v, axis=-1, keepdims=True)
        return (v - m) / jnp.sqrt(s + eps)

    def _to_tokens(v):
        B_, C_, H_, W_ = v.shape
        return v.reshape(B_, C_, H_ * W_).transpose(0, 2, 1)
    def _from_tokens(t, like):
        B_, C_, H_, W_ = like.shape
        return t.transpose(0, 2, 1).reshape(B_, C_, H_, W_)

    x = x + _L0_conv_ref(_gn(x), L0_conv_qkv_w, L0_conv_qkv_b, L0_conv_proj_w, L0_conv_proj_b, L0_conv_relative_bias)
    x = x + _L1_conv_ref(_gn(x), L1_conv_kernel)
    x = x + _L2_conv_ref(_gn(x), L2_conv_cfc, L2_conv_theta_w, L2_conv_theta_b, L2_conv_phi_w, L2_conv_phi_b, L2_conv_g_w, L2_conv_g_b, L2_conv_out_w, L2_conv_out_b)
    x = x + _L3_conv_ref(_gn(x), L3_conv_Wq, L3_conv_Wk, L3_conv_Wv, L3_conv_Wo, L3_conv_base_w, L3_conv_spline_w, L3_conv_spline_scaler)
    return x


_drawn_inputs = setup_inputs


def setup_inputs(seed=0):
    import zlib

    import numpy as np

    out = dict(_drawn_inputs(seed))
    spreads = {'L0_conv_qkv_b': (0.0, 0.1), 'L0_conv_proj_b': (0.0, 0.1)}
    factors = {'L0_conv_relative_bias': 3.136,
     'L2_conv_cfc': 4.13,
     'L2_conv_theta_b': 24.866,
     'L2_conv_phi_b': 200.0,
     'L2_conv_g_b': 8.0,
     'L2_conv_out_b': 8.0,
     'L3_conv_Wq': 5.292,
     'L3_conv_Wk': 5.243,
     'L3_conv_spline_w': 200.0}
    for name, (base, spread) in spreads.items():
        noise = np.random.default_rng([zlib.crc32(name.encode()), seed]).standard_normal(out[name].shape)
        drawn = base * np.exp(spread * noise) if base else spread * noise
        out[name] = jnp.asarray(drawn.astype(out[name].dtype))
    for name, factor in factors.items():
        out[name] = (out[name] * factor).astype(out[name].dtype)
    return out
```

```python
from contextlib import ExitStack, contextmanager

import numpy as np

import concourse.bass as bass
from concourse import mybir

F32 = mybir.dt.float32
ALU = mybir.AluOpType
ACT = mybir.ActivationFunctionType
AX = mybir.AxisListType

P = 128
B = 2
HALVES = 2
UNITS = B * HALVES
IMG = 56
L = IMG * IMG
CHUNK = 8 * IMG
CHUNKS = L // CHUNK
GN_EPS = 1e-5

WS = 7
GRID = IMG - WS + 1
KEYS = WS * WS
HEADS0 = 8
HD0 = 32
TILE = 2 * IMG
TILES = L // TILE
DY_STEP = 356
DX_STEP = 51
WIN = 4
COLS = (WS + 1) * WS * WIN
EXTRA = WS * DY_STEP
BOTTOM_SHIFT = 8
PAIR0 = 2860
CORNER0 = PAIR0 + 6 * 51
QCOLS = CORNER0 + 4 * 12
PAIR_W = 104
ONEHOT_OFF = 147
BIAS_ROWS = GRID + IMG + 2 * (TILES - 1)
ONEHOT_W = ONEHOT_OFF + BIAS_ROWS + 36
BIAS_ROW = (WS * WIN + 6 * WIN) * HEADS0
CORNER_PIX = (0, 48 * IMG + 1, 7 * IMG + 6, 55 * IMG + 7)

HEADS3 = 4
HD3 = 32
QT3 = 64
TILES3 = L // QT3
HALF = L // 2
SUB = HALF // 4
KNOT_H = 2.4
KNOT_IN, KNOT_OUT = 1.2, 3.6

W_QKV, W_PROJ, W_THETA, W_PHI, W_G, W_OUT, W_Q3, W_K3, W_V3, W_O3, W_BLOCKS = \
    0, 12, 16, 18, 20, 22, 24, 26, 28, 30, 32


def spline_matrix():
    h = KNOT_H
    m = np.zeros((8, 8))
    u3, u2, u1, one = [np.array(v) for v in ((1.0, 1.5, 0.75, 0.125), (0, 1.0, 1.0, 0.25), (0, 0, 1.0, 0.5), (0, 0, 0, 1.0))]
    pieces = {5: u3, 4: -3 * u3 + 3 * u2 + 3 * u1 + one, 3: 3 * u3 - 6 * u2 + 4 * one, 2: -u3 + 3 * u2 - 3 * u1 + one}
    for k, p in pieces.items():
        for row, power in ((0, 3), (1, 2), (2, 1), (7, 0)):
            m[row, k] = p[3 - power] / 6 / h ** power
    binom = (1, 4, 6, 4, 1)
    for j in range(5):
        c = (-1) ** j * binom[j] / (6 * h ** 3)
        m[3, j + 1] += c
        m[4, j] += c
        m[5, 6 - j] += c
        m[6, 7 - j] += c
    m[5] -= m[3]
    m[6] -= m[4]
    return m.astype(np.float32)


def window_mask():
    m = np.zeros((TILES, TILE, WS + 1, WS, WIN), np.float32)
    p = np.arange(TILE)
    col = p % IMG
    for t in range(TILES):
        row = 2 * t + p // IMG
        for w in range(WIN):
            place = 2 * t + 50 * (p // IMG) + col - KEYS * w
            for dx in range(WS):
                for dy in range(WS):
                    j = place + 6 * dy
                    m[t, :, dy, dx, w] = (j >= 0) & (j < KEYS) & (col >= dx) & (col < dx + GRID) & (row >= dy) & (row < dy + GRID)
                if 1 <= dx <= 3:
                    m[t, :, WS, dx, w] = (place >= 0) & (place < KEYS) & (col < GRID) & (row < GRID - 1)
                if dx > 3:
                    j = place + 36
                    m[t, :, WS, dx, w] = (j >= 0) & (j < KEYS) & (col >= WS - 1) & (row >= WS)
    return m.reshape(TILES, TILE, COLS)




@contextmanager
def signals(nc, tag):
    with ExitStack() as st:
        made = []

        def make(name):
            made.append(st.enter_context(nc.semaphore(f"{name}_{tag}")))
            return made[-1]
        yield make
        with nc.Block() as block:
            @block.sync
            def _(sp):
                for s in made:
                    sp.sem_clear(s)
class OnChip:
    pass


def conv_preact_kernel(nc, x, qkv_w, qkv_b, proj_w, proj_b, rel_bias, fir, cfc, theta_w, theta_b,
                       phi_w, phi_b, g_w, g_b, out_w, out_b, wq3, wk3, wv3, wo3, base_w, spline_w,
                       spline_scaler, mask_dram, spline_m, out):
    with ExitStack() as ctx:
        def sb(name, shape):
            return ctx.enter_context(nc.sbuf_tensor(name, shape, F32))

        m = OnChip()
        m.X = sb("X", [P, UNITS, L])
        m.WT = sb("WT", [P, W_BLOCKS, P])
        m.ident = sb("ident", [P, P])
        m.group = sb("group", [P, P])
        m.rstd = sb("rstd", [P, UNITS])
        m.nbias = sb("nbias", [P, UNITS])
        m.mv = sb("mv", [P, UNITS, 2])
        m.qkvb = sb("qkvb", [P, 6])
        m.pbias = sb("pbias", [P, HALVES])
        m.vbias = sb("vbias", [P, HALVES * P])
        m.rb = sb("rb", [KEYS, WS, WS, HEADS0])
        m.fir = sb("fir_taps", [P, 16])
        m.cfc = sb("cfc", [P, HALVES, 2])
        m.bias2 = sb("bias2", [P, 4])
        m.gbias = sb("gbias", [P, P])
        m.coef = sb("coef", [P, 8])
        m.smat = sb("smat", [P, 8, 8])
        m.basew = sb("basew", [P, 1])
        m.scaler = sb("scaler", [P, 1])

        m.onehot = sb("onehot", [KEYS, ONEHOT_W])
        bias_dram = nc.dram_tensor("bias_rows_dram", (BIAS_ROWS, BIAS_ROW), F32, kind="Internal").ap()

        load_and_turn(nc, m, locals())
        bias_rows0(nc, m, bias_dram)
        group_norm_stats(nc, m, "0")
        for b in range(B):
            attention0(nc, m, b, mask_dram, bias_dram)
        group_norm_stats(nc, m, "1")
        blur1(nc, m)
        group_norm_stats(nc, m, "2")
        attention2(nc, m)
        group_norm_stats(nc, m, "3")
        attention3(nc, m)

        stored = ctx.enter_context(nc.semaphore("stored"))
        with nc.Block() as block:
            @block.sync
            def _(sp):
                for u in range(UNITS):
                    sp.dma_start(out[u // 2, (u % 2) * P:(u % 2 + 1) * P].rearrange("c h w -> c (h w)"), m.X[:, u, :]).then_inc(stored, 16)
                sp.wait_ge(stored, 16 * UNITS)


def load_and_turn(nc, m, a):
    with ExitStack() as st:
        sem = st.enter_context(signals(nc, "load"))
        wnat = st.enter_context(nc.sbuf_tensor("wnat", [P, W_BLOCKS, P], F32))
        turned = [st.enter_context(nc.psum_tensor(f"turned{i}", [P, 4, P], F32)) for i in range(2)]
        x_loaded, w_loaded, small_loaded = sem("x_loaded"), sem("w_loaded"), sem("small_loaded")
        tables_made, w_turned, w_copied = sem("tables_made"), sem("w_turned"), sem("w_copied")
        with nc.Block() as block:
            @block.sync
            def _(sp):
                for w, at, blocks in ((a["qkv_w"], W_QKV, 6), (a["proj_w"], W_PROJ, 2), (a["theta_w"], W_THETA, 1),
                                      (a["phi_w"], W_PHI, 1), (a["g_w"], W_G, 1), (a["wq3"], W_Q3, 1),
                                      (a["wk3"], W_K3, 1), (a["wv3"], W_V3, 1)):
                    sp.dma_start(wnat[:, at:at + 2 * blocks, :].rearrange("p (o i) c -> p o (i c)", o=blocks),
                                 w.rearrange("(o p) c -> p o c", p=P)).then_inc(w_loaded, 16)
                for w, at in ((a["out_w"], W_OUT), (a["wo3"], W_O3)):
                    sp.dma_start(wnat[:, at:at + 2, :], w.rearrange("(o p) c -> p o c", p=P)).then_inc(w_loaded, 16)
                for u in range(UNITS):
                    sp.dma_start(m.X[:, u, :], a["x"][u // 2, (u % 2) * P:(u % 2 + 1) * P].rearrange("c h w -> c (h w)")).then_inc(x_loaded, 16)
                sp.wait_ge(x_loaded, 16 * UNITS)

            @block.scalar
            def _(act):
                smalls = [(m.qkvb[:, :], a["qkv_b"].rearrange("(o p) -> p o", p=P)),
                          (m.pbias[:, :], a["proj_b"].rearrange("(o p) -> p o", p=P)),
                          (m.vbias[:, :], a["qkv_b"][2 * HALVES * P:].partition_broadcast(P)),
                          (m.fir[:, :], a["fir"].rearrange("a b -> (a b)").partition_broadcast(P)),
                          (m.cfc[:, :, :], a["cfc"].rearrange("(o p) t -> p o t", p=P)),
                          (m.bias2[:, 0:1], a["theta_b"].rearrange("(p o) -> p o", o=1)),
                          (m.bias2[:, 1:2], a["phi_b"].rearrange("(p o) -> p o", o=1)),
                          (m.bias2[:, 2:4], a["out_b"].rearrange("(o p) -> p o", p=P)),
                          (m.gbias[:, :], a["g_b"].partition_broadcast(P)),
                          (m.coef[:, :], a["spline_w"].rearrange("a b k -> (a b k)").partition_broadcast(P)),
                          (m.smat[:, :, :].rearrange("p a b -> p (a b)"), a["spline_m"].rearrange("a b -> (a b)").partition_broadcast(P)),
                          (m.basew[:, :], a["base_w"].rearrange("a b -> (a b)").partition_broadcast(P)),
                          (m.scaler[:, :], a["spline_scaler"].rearrange("a b -> (a b)").partition_broadcast(P))]
                for kh in range(WS):
                    smalls.append((m.rb[kh * WS:(kh + 1) * WS].rearrange("k a b h -> k a (b h)"),
                                   bass.AP(a["rel_bias"].tensor, kh * (2 * WS - 1) * HEADS0,
                                           [[HEADS0, WS], [(2 * WS - 1) * HEADS0, WS], [1, WS * HEADS0]])))
                for dst, src in smalls:
                    act.dma_start(dst, src, allow_slow_non_contiguous=True).then_inc(small_loaded, 16)
                act.wait_ge(small_loaded, 16 * len(smalls))

            @block.gpsimd
            def _(pool):
                pool.memset(m.ident[:, :], 0.0).then_inc(tables_made, 1)
                pool.memset(m.group[:, :], 1.0 / 8).then_inc(tables_made, 1)
                pool.wait_ge(tables_made, 2)
                pool.affine_select(out=m.ident[:, :], in_=m.ident[:, :], compare_op=ALU.not_equal, fill=1.0, base=0,
                                   pattern=[[-1, P]], channel_multiplier=1).then_inc(tables_made, 1)
                g3 = m.group[:, :].rearrange("p (g c) -> p g c", c=8)
                pool.affine_select(out=g3, in_=g3, compare_op=ALU.is_ge, fill=0.0, base=0,
                                   pattern=[[-8, 16], [0, 8]], channel_multiplier=1).then_inc(tables_made, 1)
                pool.wait_ge(tables_made, 4)
                pool.affine_select(out=g3, in_=g3, compare_op=ALU.is_ge, fill=0.0, base=7,
                                   pattern=[[8, 16], [0, 8]], channel_multiplier=-1).then_inc(tables_made, 1)
                pool.wait_ge(tables_made, 5)

            @block.tensor
            def _(pe):
                pe.wait_ge(tables_made, 5)
                pe.wait_ge(w_loaded, 160)
                for n in range(W_BLOCKS // 4):
                    if n >= 2:
                        pe.wait_ge(w_copied, n - 1)
                    for j in range(4):
                        t = pe.transpose(turned[n % 2][:, j, :], wnat[:, 4 * n + j, :], m.ident[:, :])
                    t.then_inc(w_turned, 1)

            @block.vector
            def _(dve):
                for n in range(W_BLOCKS // 4):
                    dve.wait_ge(w_turned, n + 1)
                    dve.tensor_copy(m.WT[:, 4 * n:4 * n + 4, :], turned[n % 2][:, :, :]).then_inc(w_copied, 1)
                dve.wait_ge(w_copied, W_BLOCKS // 4)


def group_norm_stats(nc, m, tag):
    with ExitStack() as st:
        sem = st.enter_context(signals(nc, tag))
        sb = lambda name, shape: st.enter_context(nc.sbuf_tensor(name + tag, shape, F32))
        stats = sb("stats", [P, UNITS, CHUNKS, 6])
        sq = sb("sq", [P, UNITS])
        e2 = sb("e2", [P, UNITS, 2])
        gst = sb("gst", [P, UNITS, 2])
        gsq = sb("gsq", [P, UNITS])
        gvar = sb("gvar", [P, UNITS])
        geps = sb("geps", [P, UNITS])
        gstd = sb("gstd", [P, UNITS])
        gp = st.enter_context(nc.psum_tensor("gp" + tag, [P, 2 * UNITS], F32))
        chain, moments, grouped, var_ready, std_ready = (sem(n) for n in ("gn_chain", "gn_moments", "gn_grouped", "gn_var", "gn_std"))
        with nc.Block() as block:
            @block.vector
            def _(dve):
                done = [0]

                def link(ins):
                    done[0] += 1
                    ins.then_inc(chain, 1)

                for u in range(UNITS):
                    for k in range(CHUNKS):
                        link(dve.bn_stats(stats[:, u, k, :], m.X[:, u, CHUNK * k:CHUNK * (k + 1)]))
                dve.wait_ge(chain, done[0])
                for u in range(UNITS):
                    link(dve.bn_aggr(m.mv[:, u, :], stats[:, u, :, :].rearrange("p k s -> p (k s)")))
                dve.wait_ge(chain, done[0])
                link(dve.tensor_tensor(sq[:, :], m.mv[:, :, 0], m.mv[:, :, 0], ALU.mult))
                dve.wait_ge(chain, done[0])
                dve.tensor_copy(e2[:, :, 0], m.mv[:, :, 0]).then_inc(moments, 1)
                dve.tensor_tensor(e2[:, :, 1], sq[:, :], m.mv[:, :, 1], ALU.add).then_inc(moments, 1)
                dve.wait_ge(grouped, 1)
                link(dve.tensor_copy(gst[:, :, :].rearrange("p u s -> p (u s)"), gp[:, :]))
                dve.wait_ge(chain, done[0])
                link(dve.tensor_tensor(gsq[:, :], gst[:, :, 0], gst[:, :, 0], ALU.mult))
                dve.wait_ge(chain, done[0])
                link(dve.tensor_tensor(gvar[:, :], gst[:, :, 1], gsq[:, :], ALU.subtract))
                dve.wait_ge(chain, done[0])
                dve.tensor_scalar(geps[:, :], gvar[:, :], GN_EPS, None, ALU.add).then_inc(var_ready, 1)
                dve.wait_ge(std_ready, 1)
                link(dve.reciprocal(m.rstd[:, :], gstd[:, :]))
                dve.wait_ge(chain, done[0])
                link(dve.scalar_tensor_tensor(m.nbias[:, :], gst[:, :, 0], -1.0, m.rstd[:, :], ALU.mult, ALU.mult))
                dve.wait_ge(chain, done[0])

            @block.tensor
            def _(pe):
                pe.wait_ge(moments, 2)
                pe.matmul(gp[:, :], m.group[:, :], e2[:, :, :].rearrange("p u s -> p (u s)"), start=True, stop=True).then_inc(grouped, 1)

            @block.scalar
            def _(act):
                act.wait_ge(var_ready, 1)
                act.activation(gstd[:, :], geps[:, :], ACT.Sqrt).then_inc(std_ready, 1)
                act.wait_ge(std_ready, 1)


def bias_rows0(nc, m, bias_dram):
    with ExitStack() as st:
        sem = st.enter_context(signals(nc, "bias"))
        rows = [st.enter_context(nc.sbuf_tensor(f"bias_rows{k}", [P, BIAS_ROW], F32)) for k in range(2)]
        rp = [st.enter_context(nc.psum_tensor(f"bias_rows_psum{k}", [P, 512], F32)) for k in range(2)]
        table, laid_out, copied, stored = sem("onehot_made"), sem("bias_laid_out"), sem("bias_rows_copied"), sem("bias_rows_stored")
        blocks = ((0, P), (P, BIAS_ROWS - P))
        with nc.Block() as block:
            @block.gpsimd
            def _(pool):
                pool.memset(m.onehot[:, :], 0.0).then_inc(table, 1)
                pool.wait_ge(table, 1)
                pool.affine_select(out=m.onehot[:, :], in_=m.onehot[:, :], compare_op=ALU.not_equal, fill=1.0, base=-ONEHOT_OFF,
                                   pattern=[[1, ONEHOT_W]], channel_multiplier=-1).then_inc(table, 1)

            @block.tensor
            def _(pe):
                pe.wait_ge(table, 2)
                for k, (u0, nu) in enumerate(blocks):
                    def place(s):
                        return m.onehot[:, ONEHOT_OFF + u0 + s:ONEHOT_OFF + u0 + s + nu]
                    for dy in range(WS):
                        for w in range(WIN):
                            at = (dy * WIN + w) * HEADS0
                            pe.matmul(rp[k][0:nu, at:at + HEADS0], place(6 * dy - KEYS * w), m.rb[:, 3, 3, :], start=True, stop=True)
                    for w in range(WIN):
                        for side in range(2):
                            at = (WS * WIN + w * 6 + 3 * side) * HEADS0
                            mm = pe.matmul(rp[k][0:nu, at:at + 3 * HEADS0], place(36 * side - KEYS * w),
                                           m.rb[:, 4 * side:4 * side + 3, 3, :], start=True, stop=True)
                    mm.then_inc(laid_out, 1)

            @block.vector
            def _(dve):
                for k, (u0, nu) in enumerate(blocks):
                    dve.wait_ge(laid_out, k + 1)
                    dve.tensor_copy(rows[k][0:nu, :], rp[k][0:nu, 0:BIAS_ROW]).then_inc(copied, 1)

            @block.sync
            def _(sp):
                for k, (u0, nu) in enumerate(blocks):
                    sp.wait_ge(copied, k + 1)
                    sp.dma_start(bias_dram[u0:u0 + nu, :], rows[k][0:nu, :]).then_inc(stored, 16)
                sp.wait_ge(stored, 32)


def attention0(nc, m, b, mask_dram, bias_dram):
    scale = float(HD0) ** -0.5
    with ExitStack() as outer:
        keep = lambda name, shape: outer.enter_context(nc.sbuf_tensor(f"{name}_{b}", shape, F32))
        xn = keep("xn0", [P, HALVES, L])
        Q = keep("Q0", [P, HALVES, QCOLS])
        O = keep("O0", [P, HALVES, QCOLS])
        qb = keep("qb0", [P, HALVES])

        project_queries0(nc, m, b, xn, Q, O, qb, scale)
        row_pairs0(nc, m, b, xn, Q, O, mask_dram, bias_dram)
        border0(nc, m, b, xn, Q, O)
        project_out0(nc, m, b, O)


def project_queries0(nc, m, b, xn, Q, O, qb, scale):
    with ExitStack() as st:
        sem = st.enter_context(signals(nc, f"p0_{b}"))
        qp = [st.enter_context(nc.psum_tensor(f"qp{i}_{b}", [P, 8, IMG], F32)) for i in range(4)]
        normed, cleared, q_made, q_placed, qb_ready = (sem(n) for n in ("xn_ready", "cleared", "q_made", "q_placed", "qb_ready"))
        with nc.Block() as block:
            @block.vector
            def _(dve):
                for i in range(HALVES):
                    u = HALVES * b + i
                    dve.tensor_scalar(xn[:, i, :], m.X[:, u, :], m.rstd[:, u:u + 1], m.nbias[:, u:u + 1], ALU.mult, ALU.add).then_inc(normed, 1)
                dve.tensor_scalar(qb[:, :], m.qkvb[:, 0:2], scale, None, ALU.mult).then_inc(qb_ready, 1)
                dve.memset(O[:, :, :], 0.0).then_inc(cleared, 1)

            @block.gpsimd
            def _(pool):
                pool.memset(Q[:, :, GRID * GRID:PAIR0 + 6], 0.0).then_inc(cleared, 1)
                pool.memset(Q[:, :, CORNER0 - 6:CORNER0], 0.0).then_inc(cleared, 1)

            @block.tensor
            def _(pe):
                pe.wait_ge(normed, HALVES)
                for n in range(HALVES * CHUNKS):
                    k, o = n // HALVES, n % HALVES
                    if n >= 4:
                        pe.wait_ge(q_placed, n - 3)
                    for i in range(HALVES):
                        mm = pe.matmul(qp[n % 4][:, :, :].rearrange("p r c -> p (r c)"), m.WT[:, W_QKV + 2 * o + i, :],
                                       xn[:, i, CHUNK * k:CHUNK * (k + 1)], start=(i == 0), stop=(i == HALVES - 1))
                    mm.then_inc(q_made, 1)

            @block.scalar
            def _(act):
                act.wait_ge(qb_ready, 1)
                act.wait_ge(cleared, 3)
                for n in range(HALVES * CHUNKS):
                    k, o = n // HALVES, n % HALVES
                    act.wait_ge(q_made, n + 1)
                    placed = [None]

                    def place(dst, rows, cols):
                        src = qp[n % 4][:, rows[0] - 8 * k:rows[1] - 8 * k, cols[0]:cols[1]]
                        placed[0] = act.activation(dst, src, ACT.Identity, bias=qb[:, o:o + 1], scale=scale)

                    def span(at, rows, row_step, cols):
                        return Q[:, o, at:at + rows * row_step].rearrange("p (r c) -> p r c", c=row_step)[:, :, 0:cols]

                    r0, r1 = max(3, 8 * k), min(53, 8 * k + 8)
                    place(span((r0 - 3) * GRID, r1 - r0, GRID, GRID), (r0, r1), (3, 53))
                    place(span(PAIR0 + 6 * (r0 - 3) + 3, r1 - r0, 6, 3), (r0, r1), (0, 3))
                    place(span(PAIR0 + 6 * (r0 - 2), r1 - r0, 6, 3), (r0, r1), (53, 56))
                    if k == 0:
                        place(span(EXTRA + DX_STEP, 3, DX_STEP, GRID), (0, 3), (3, 53))
                        place(span(CORNER0, 4, 3, 3), (0, 4), (0, 3))
                        place(span(CORNER0 + 12, 4, 3, 3), (0, 4), (53, 56))
                    if k == CHUNKS - 1:
                        place(span(EXTRA + 4 * DX_STEP + BOTTOM_SHIFT, 3, DX_STEP, GRID), (53, 56), (3, 53))
                        place(span(CORNER0 + 24, 4, 3, 3), (52, 56), (0, 3))
                        place(span(CORNER0 + 36, 4, 3, 3), (52, 56), (53, 56))
                    placed[0].then_inc(q_placed, 1)
                act.wait_ge(q_placed, HALVES * CHUNKS)


def row_pairs0(nc, m, b, xn, Q, O, mask_dram, bias_dram):
    with ExitStack() as st:
        sem = st.enter_context(signals(nc, f"a0_{b}"))
        sb = lambda name, shape: st.enter_context(nc.sbuf_tensor(f"{name}_{b}", shape, F32))
        ps = lambda name, shape: st.enter_context(nc.psum_tensor(f"{name}_{b}", shape, F32))
        xt = [sb(f"xt{r}", [P, HALVES, TILE]) for r in range(2)]
        qt = [sb(f"qt{r}", [P, HALVES, COLS]) for r in range(2)]
        kt = [sb(f"kt{r}", [P, HALVES, TILE]) for r in range(2)]
        vt = [sb(f"vt{r}", [TILE, HALVES * P]) for r in range(2)]
        rows = [sb(f"rows{r}", [TILE, BIAS_ROW]) for r in range(2)]
        mask = [sb(f"mask{r}", [TILE, COLS]) for r in range(2)]
        bias = [sb(f"bias{r}", [TILE, 4, HALVES, COLS]) for r in range(2)]
        A = [sb(f"A{r}", [TILE, 4, HALVES, COLS]) for r in range(2)]
        kvp = [ps(f"kvp{r}", [P, 512]) for r in range(2)]
        scp = ps("scp", [P, 4, 512])
        op = ps("op", [P, 512])
        xt_ready, qt_ready, kv_ready, bias_ready, scores_made, o_made, o_added, bias_zeroed = (
            sem(n) for n in ("xt_ready", "qt_ready", "kv_ready", "bias_ready", "scores_made", "o_made", "o_added", "bias_zeroed"))
        tables_loaded = [sem(f"tables_loaded{r}") for r in range(2)]
        kv_made, scores_added, masked = (sem(n) for n in ("kv_made", "scores_added", "masked"))

        def ramp(eng, front, back):
            front(eng, 0, 0, 0)
            with eng.Fori(0, (TILES - 2) // 2) as i:
                for k in (1, 2):
                    front(eng, 2 * i + k, k % 2, i + k // 2)
                    back(eng, 2 * i + (k - 1), (k - 1) % 2, i)
            front(eng, TILES - 1, 1, TILES // 2 - 1)
            back(eng, TILES - 2, 0, TILES // 2 - 1)
            back(eng, TILES - 1, 1, TILES // 2 - 1)

        def nothing(eng, t, r, turn):
            pass

        def block_cols(view, t):
            return bass.AP(view.tensor, view.offset + 2 * t, [view.ap[0], [DY_STEP, WS + 1], [DX_STEP, WS], [1, WIN]])

        def fixed_cols(view):
            return view.rearrange("p (y x w) -> p y x w", y=WS + 1, x=WS)

        with nc.Block() as block:
            @block.sync
            def _(sp):
                def load(eng, t, r, turn):
                    eng.wait_ge(masked, t + 1)
                    eng.dma_start(mask[r][:, :], mask_dram[bass.ds(t, 1)].rearrange("t p c -> p (t c)")).then_inc(tables_loaded[r], 16)
                    eng.wait_ge(bias_ready, t + 1)
                    for q in range(2):
                        eng.dma_start(rows[r][q * IMG:(q + 1) * IMG, :], bias_dram[bass.ds(2 * t + GRID * q, IMG), :]).then_inc(tables_loaded[r], 16)
                ramp(sp, load, nothing)

            @block.scalar
            def _(act):
                def stage(eng, t, r, turn):
                    eng.wait_ge(kv_made, t + 1)
                    eng.activation(xt[r][:, :, :], xn[:, :, bass.ds(TILE * t, TILE)], ACT.Copy).then_inc(xt_ready, 1)
                    eng.wait_ge(tables_loaded[r], 48 * (turn + 1))
                    eng.wait_ge(scores_added, t + 1)
                    for h in range(4):
                        for f in range(HALVES):
                            dst = bias[r][:, h, f, 0:WS * WS * WIN].rearrange("p (y x w) -> p y x w", y=WS, x=WS)
                            src = rows[r][:, 0:WS * WIN * HEADS0].rearrange("p (y w e) -> p y w e", y=WS, w=WIN)[:, :, :, 4 * f + h]
                            eng.activation(dst, src.unsqueeze(2).to_broadcast([TILE, WS, WS, WIN]), ACT.Copy)
                    for f in range(HALVES):
                        for w in range(WIN):
                            dst = bias[r][:, :, f, WS * WS * WIN:].rearrange("p h (x w) -> p h x w", w=WIN)[:, :, 1:WS, w]
                            at = WS * WIN * HEADS0 + w * 6 * HEADS0
                            src = rows[r][:, at:at + 6 * HEADS0].rearrange("p (s e) -> p e s", e=HEADS0)[:, 4 * f:4 * f + 4, :]
                            last = eng.activation(dst, src, ACT.Copy)
                    last.then_inc(bias_ready, 1)
                act.wait_ge(bias_zeroed, 2)
                ramp(act, stage, nothing)

            @block.gpsimd
            def _(pool):
                def stage(eng, t, r, turn):
                    eng.wait_ge(scores_added, t + 1)
                    for f in range(HALVES):
                        eng.tensor_copy(fixed_cols(qt[r][:, f, :]), block_cols(Q[:, f, :], t)).then_inc(qt_ready, 1)

                def apply_mask(eng, t, r, turn):
                    eng.wait_ge(tables_loaded[r], 48 * (turn + 1))
                    eng.wait_ge(scores_added, t + 3)
                    a = A[r][:, :, :, :].rearrange("p h f c -> p (h f) c")
                    eng.tensor_tensor(a, a, mask[r][:, :].unsqueeze(1).to_broadcast([TILE, 8, COLS]), ALU.mult).then_inc(masked, 1)

                pool.sem_inc(masked, 2)
                for r in range(2):
                    pool.memset(bias[r][:, :, :, WS * WS * WIN:].rearrange("p h f c -> p (h f) c"), 0.0).then_inc(bias_zeroed, 1)
                ramp(pool, stage, apply_mask)

            @block.tensor
            def _(pe):
                def front(eng, t, r, turn):
                    eng.wait_ge(xt_ready, t + 1)
                    eng.wait_ge(kv_ready, 3 * (t + 1))
                    for f in range(HALVES):
                        for i in range(HALVES):
                            eng.matmul(kvp[r][:, f * TILE:(f + 1) * TILE], m.WT[:, W_QKV + 2 * (2 + f) + i, :], xt[r][:, i, :],
                                       start=(i == 0), stop=(i == HALVES - 1))
                    for i in range(HALVES):
                        mm = eng.matmul(kvp[r][0:TILE, 2 * TILE:2 * TILE + 2 * P], xt[r][:, i, :],
                                        m.WT[:, W_QKV + 8 + i:W_QKV + 12:2, :], start=(i == 0), stop=(i == HALVES - 1))
                    mm.then_inc(kv_made, 1)
                    eng.wait_ge(kv_ready, 3 * (t + 3))
                    eng.wait_ge(qt_ready, HALVES * (t + 1))
                    eng.wait_ge(scores_added, t + 2)
                    for f in range(HALVES):
                        for h in range(4):
                            rows = slice(HD0 * h, HD0 * (h + 1))
                            mm = eng.matmul(scp[0:TILE, h, f * COLS:(f + 1) * COLS], kt[r][rows, f, :], qt[r][rows, f, :], start=True, stop=True)
                    mm.then_inc(scores_made, 1)

                def back(eng, t, r, turn):
                    eng.wait_ge(masked, t + 3)
                    eng.wait_ge(o_added, HALVES * (t + 1))
                    for f in range(HALVES):
                        for h in range(4):
                            rows = slice(HD0 * h, HD0 * (h + 1))
                            mm = eng.matmul(op[rows, f * COLS:(f + 1) * COLS], vt[r][:, f * P + HD0 * h:f * P + HD0 * (h + 1)],
                                            A[r][:, h, f, :], start=True, stop=True)
                    mm.then_inc(o_made, 1)

                pe.sem_inc(kv_made, 2)
                ramp(pe, front, back)

            @block.vector
            def _(dve):
                def front(eng, t, r, turn):
                    eng.wait_ge(kv_made, t + 3)
                    for f in range(HALVES):
                        eng.tensor_scalar(kt[r][:, f, :], kvp[r][:, f * TILE:(f + 1) * TILE], m.qkvb[:, 2 + f:3 + f], None, ALU.add).then_inc(kv_ready, 1)
                    eng.tensor_tensor(vt[r][:, :], kvp[r][0:TILE, 2 * TILE:2 * TILE + 2 * P], m.vbias[0:TILE, :], ALU.add).then_inc(kv_ready, 1)
                    eng.wait_ge(scores_made, t + 1)
                    eng.wait_ge(bias_ready, t + 3)
                    eng.tensor_tensor(A[r][:, :, :, :].rearrange("p h f c -> p h (f c)"), scp[0:TILE, :, 0:HALVES * COLS],
                                      bias[r][:, :, :, :].rearrange("p h f c -> p h (f c)"), ALU.add).then_inc(scores_added, 1)

                def back(eng, t, r, turn):
                    eng.wait_ge(o_made, t + 1)
                    eng.wait_ge(o_added, HALVES * (t + 1))
                    for f in range(HALVES):
                        dst = block_cols(O[:, f, :], t)
                        eng.tensor_tensor(dst, dst, fixed_cols(op[:, f * COLS:(f + 1) * COLS]), ALU.add).then_inc(o_added, 1)

                dve.sem_inc(kv_ready, 6)
                dve.sem_inc(scores_added, 2)
                dve.sem_inc(o_added, HALVES)
                dve.sem_inc(bias_ready, 2)
                ramp(dve, front, back)
                dve.wait_ge(o_added, HALVES * (TILES + 1))


def border0(nc, m, b, xn, Q, O):
    with ExitStack() as st:
        sem = st.enter_context(signals(nc, f"a0_{b}"))
        sb = lambda name, shape: st.enter_context(nc.sbuf_tensor(f"{name}_{b}", shape, F32))
        ps = lambda name, shape: st.enter_context(nc.psum_tensor(f"{name}_{b}", shape, F32))
        n7 = WS * PAIR_W
        xe = sb("xe", [P, HALVES, n7])
        ke = sb("ke", [P, HALVES, n7])
        ve = sb("ve", [PAIR_W, 8, HALVES * P])
        qe = sb("qe", [P, HALVES, 48])
        ae = sb("ae", [PAIR_W, 4, WS, 12])
        emask = sb("emask", [PAIR_W, HALVES, 2, 3])
        ebias = sb("ebias", [PAIR_W, 4, HALVES, 6])
        cbias = sb("cbias", [KEYS, 4, 4, HALVES, 12])
        ca = sb("ca", [KEYS, 4, 4, HALVES, 12])
        kp = ps("kpe", [P, 4, 512])
        vp = ps("vpe", [P, 4, 512])
        eb_made, eb_ready, mask_made, xe_ready, qe_ready, kv_made, kv_ready, s_made, s_masked, a_ready, o_made, o_placed = (
            sem("e_" + n) for n in ("eb_made", "eb_ready", "mask_made", "xe_ready", "qe_ready", "kv_made", "kv_ready", "s_made", "s_masked", "a_ready", "o_made", "o_placed"))
        GROUPS = WS + 1

        def k_parts(total):
            return [(0, total)] if total <= 512 else [(0, total // 2), (total // 2, total)]

        with nc.Block() as block:
            @block.gpsimd
            def _(pool):
                pool.memset(emask[:, :, :, :].rearrange("p f s q -> p (f s q)"), 1.0).then_inc(mask_made, 1)
                pool.wait_ge(mask_made, 1)
                left, right = emask[:, :, 1, :], emask[:, :, 0, :]
                pool.affine_select(out=right, in_=right, compare_op=ALU.is_ge, fill=0.0, base=KEYS - 1, pattern=[[0, HALVES], [0, 3]],
                                   channel_multiplier=-1).then_inc(mask_made, 1)
                pool.affine_select(out=left, in_=left, compare_op=ALU.is_ge, fill=0.0, base=-(IMG - 1), pattern=[[0, HALVES], [0, 3]],
                                   channel_multiplier=1).then_inc(mask_made, 1)

            @block.scalar
            def _(act):
                def group(eng, g, n, width, nq, xsrc, qat):
                    eng.activation(xe[:, :, 0:n * width].rearrange("p f (n w) -> p f n w", n=n), xsrc, ACT.Copy).then_inc(xe_ready, 1)
                    eng.activation(qe[:, :, 0:n * nq], Q[:, :, bass.ds(qat, n * nq)], ACT.Copy).then_inc(qe_ready, 1)
                    eng.wait_ge(o_made, g + 1)
                    src = vp[:, 0, 0:HALVES * n * nq].rearrange("p (f q) -> p f q", f=HALVES)
                    eng.activation(O[:, :, bass.ds(qat, n * nq)], src, ACT.Copy).then_inc(o_placed, 1)

                view = xn[:, :, :]
                with act.Fori(0, WS) as dy:
                    src = bass.AP(view.tensor, view.offset + (48 * IMG + 1 - 55 * (WS - 1)) - 336 * dy, [view.ap[0], [L, HALVES], [IMG - 1, WS], [1, PAIR_W]])
                    group(act, dy, WS, PAIR_W, 6, src, PAIR0 + 6 + 42 * dy)
                for c in range(4):
                    act.activation(xe[:, :, c * KEYS:(c + 1) * KEYS], xn[:, :, CORNER_PIX[c]:CORNER_PIX[c] + KEYS], ACT.Copy).then_inc(xe_ready, 1)
                act.activation(qe[:, :, :], Q[:, :, CORNER0:CORNER0 + 48], ACT.Copy).then_inc(qe_ready, 1)
                act.wait_ge(o_made, GROUPS)
                act.activation(O[:, :, CORNER0:CORNER0 + 48], vp[:, 0, 0:96].rearrange("p (f q) -> p f q", f=HALVES), ACT.Copy).then_inc(o_placed, 1)
                act.wait_ge(o_placed, GROUPS)

            @block.tensor
            def _(pe):
                for side in range(2):
                    at = ONEHOT_OFF - (IMG - 1) * side
                    c0 = 4 - 4 * side
                    mm = pe.matmul(kp[0:PAIR_W, 0, 24 * side:24 * side + 24], m.onehot[:, at:at + PAIR_W], m.rb[:, 3, c0:c0 + 3, :], start=True, stop=True)
                for c in range(4):
                    r0, c0 = 3 * (c // 2), 4 * (c % 2)
                    mm = pe.matmul(vp[0:KEYS, 0, 96 * c:96 * c + 96], m.onehot[:, ONEHOT_OFF:ONEHOT_OFF + KEYS],
                                   m.rb[:, r0:r0 + 4, c0:c0 + 3, :].rearrange("k a b h -> k a (b h)"), start=True, stop=True)
                mm.then_inc(eb_made, 1)
                pe.wait_ge(eb_ready, 5)

                def group(eng, g, n, width, nq, xe_count):
                    eng.wait_ge(xe_ready, xe_count)
                    parts = k_parts(n * width)
                    slot = lambda w: n - 1 - w if nq == 6 else w
                    for f in range(HALVES):
                        for j, (a, z) in enumerate(parts):
                            for i in range(HALVES):
                                eng.matmul(kp[:, 2 * f + j, 0:z - a], m.WT[:, W_QKV + 2 * (2 + f) + i, :], xe[:, i, a:z],
                                           start=(i == 0), stop=(i == HALVES - 1))
                    for w in range(n):
                        for i in range(HALVES):
                            mm = eng.matmul(vp[0:width, w // 2, 2 * P * (w % 2):2 * P * (w % 2 + 1)], xe[:, i, w * width:(w + 1) * width],
                                            m.WT[:, W_QKV + 8 + i:W_QKV + 12:2, :], start=(i == 0), stop=(i == HALVES - 1))
                    mm.then_inc(kv_made, 1)
                    eng.wait_ge(qe_ready, g + 1)
                    eng.wait_ge(kv_ready, g + 1)
                    for w in range(n):
                        for f in range(HALVES):
                            for h in range(4):
                                rows = slice(HD0 * h, HD0 * (h + 1))
                                at = (w * HALVES + f) * nq
                                mm = eng.matmul(kp[0:width, h, at:at + nq], ke[rows, f, slot(w) * width:(slot(w) + 1) * width],
                                                qe[rows, f, w * nq:(w + 1) * nq], start=True, stop=True)
                    mm.then_inc(s_made, 1)
                    eng.wait_ge(a_ready, g + 1)
                    for w in range(n):
                        for f in range(HALVES):
                            for h in range(4):
                                rows = slice(HD0 * h, HD0 * (h + 1))
                                rhs = ae[:, h, w, f * nq:(f + 1) * nq] if nq == 6 else ca[:, h, w, f, :]
                                at = f * n * nq + w * nq
                                mm = eng.matmul(vp[rows, 0, at:at + nq], ve[0:width, slot(w), f * P + HD0 * h:f * P + HD0 * (h + 1)], rhs, start=True, stop=True)
                    mm.then_inc(o_made, 1)
                    eng.wait_ge(o_placed, g + 1)

                with pe.Fori(0, WS) as dy:
                    group(pe, dy, WS, PAIR_W, 6, dy + 1)
                group(pe, WS, 4, KEYS, 12, WS + 4)

            @block.vector
            def _(dve):
                dve.wait_ge(eb_made, 1)
                dve.tensor_copy(ebias[:, :, :, :], kp[0:PAIR_W, 0, 0:48].rearrange("p (q f h) -> p h f q", q=6, f=HALVES)).then_inc(eb_ready, 1)
                for c in range(4):
                    src = vp[0:KEYS, 0, 96 * c:96 * c + 96].rearrange("p (q f h) -> p h f q", q=12, f=HALVES)
                    dve.tensor_copy(cbias[:, :, c, :, :], src).then_inc(eb_ready, 1)
                dve.wait_ge(eb_ready, 5)
                dve.wait_ge(mask_made, 3)

                def kv(eng, g, n, width):
                    eng.wait_ge(kv_made, g + 1)
                    for f in range(HALVES):
                        for j, (a, z) in enumerate(k_parts(n * width)):
                            eng.tensor_scalar(ke[:, f, a:z], kp[:, 2 * f + j, 0:z - a], m.qkvb[:, 2 + f:3 + f], None, ALU.add)
                    eng.tensor_tensor(ve[0:width, 0:n, :], vp[0:width, :, :].rearrange("p a (b c) -> p (a b) c", b=2)[:, 0:n, :],
                                      m.vbias[0:width, :].unsqueeze(1).to_broadcast([width, n, HALVES * P]), ALU.add).then_inc(kv_ready, 1)

                with dve.Fori(0, WS) as dy:
                    kv(dve, dy, WS, PAIR_W)
                    dve.wait_ge(s_made, dy + 1)
                    dve.tensor_tensor(ae[:, :, :, :], kp[0:PAIR_W, :, 0:84].rearrange("p h (w c) -> p h w c", w=WS),
                                      emask[:, :, :, :].rearrange("p f s q -> p (f s q)").unsqueeze(1).unsqueeze(1).to_broadcast([PAIR_W, 4, WS, 12]),
                                      ALU.mult).then_inc(s_masked, 1)
                    dve.wait_ge(s_masked, dy + 1)
                    dve.tensor_tensor(ae[:, :, :, :], ae[:, :, :, :],
                                      ebias[:, :, :, :].rearrange("p h f q -> p h (f q)").unsqueeze(2).to_broadcast([PAIR_W, 4, WS, 12]),
                                      ALU.add).then_inc(a_ready, 1)
                kv(dve, WS, 4, KEYS)
                dve.wait_ge(s_made, GROUPS)
                dve.tensor_tensor(ca[:, :, :, :, :].rearrange("p h c f q -> p h (c f q)"), kp[0:KEYS, :, 0:96],
                                  cbias[:, :, :, :, :].rearrange("p h c f q -> p h (c f q)"), ALU.add).then_inc(a_ready, 1)


def project_out0(nc, m, b, O):
    with ExitStack() as st:
        sem = st.enter_context(signals(nc, f"p0_{b}"))
        yp = [st.enter_context(nc.psum_tensor(f"yp{i}_{b}", [P, 512], F32)) for i in range(8)]
        y_made, y_added = sem("y_made"), sem("y_added")
        slots = EXTRA + DX_STEP
        spans = [(500 * k, 500) for k in range(5)] + [(slots, 314), (PAIR0 + 6, 294), (CORNER0, 48)]
        with nc.Block() as block:
            @block.tensor
            def _(pe):
                for n in range(2 * len(spans)):
                    f, (at, w) = n % 2, spans[n // 2]
                    if n >= 8:
                        pe.wait_ge(y_added, n - 7)
                    for i in range(HALVES):
                        mm = pe.matmul(yp[n % 8][:, 0:w], m.WT[:, W_PROJ + 2 * f + i, :], O[:, i, at:at + w], start=(i == 0), stop=(i == 1))
                    mm.then_inc(y_made, 1)

            @block.vector
            def _(dve):
                for n in range(2 * len(spans)):
                    f, k = n % 2, n // 2
                    dve.wait_ge(y_made, n + 1)
                    X = m.X[:, HALVES * b + f, :]
                    img = X.rearrange("p (r c) -> p r c", c=IMG)
                    last = [None]

                    def add(dst, src):
                        last[0] = dve.scalar_tensor_tensor(dst, src, m.pbias[:, f:f + 1], dst, ALU.add, ALU.add)

                    def grid(at, rows, step, cols):
                        return yp[n % 8][:, at:at + rows * step].rearrange("p (r c) -> p r c", c=step)[:, :, 0:cols]

                    if k < 5:
                        add(img[:, 3 + 10 * k:13 + 10 * k, 3:53], grid(0, 10, GRID, GRID))
                    elif k == 5:
                        add(img[:, 0:3, 3:53], grid(0, 3, DX_STEP, GRID))
                        add(img[:, 53:56, 3:53], grid(3 * DX_STEP + BOTTOM_SHIFT, 3, DX_STEP, GRID))
                    elif k == 6:
                        add(X[:, 3 * IMG + 53:3 * IMG + 53 + 49 * IMG].rearrange("p (r c) -> p r c", c=IMG)[:, :, 0:6], grid(0, 49, 6, 6))
                    else:
                        add(img[:, 0:4, 0:3], grid(0, 4, 3, 3))
                        add(img[:, 0:3, 53:56], grid(12, 3, 3, 3))
                        add(img[:, 53:56, 0:3], grid(27, 3, 3, 3))
                        add(img[:, 52:56, 53:56], grid(36, 4, 3, 3))
                    last[0].then_inc(y_added, 1)
                dve.wait_ge(y_added, 2 * len(spans))


def blur1(nc, m):
    PAD, KW = 2, 4
    W = IMG + PAD + 1
    with ExitStack() as st:
        sem = st.enter_context(signals(nc, "blur"))
        pad = [st.enter_context(nc.sbuf_tensor(f"pad{r}", [P, W, W], F32)) for r in range(2)]
        cleared, padded, tapped, rows_done = sem("pad_cleared"), sem("padded"), sem("tapped"), sem("unit_blurred")
        with nc.Block() as block:
            @block.gpsimd
            def _(pool):
                for r in range(2):
                    pool.memset(pad[r][:, :, :], 0.0).then_inc(cleared, 1)

            @block.scalar
            def _(act):
                for u in range(UNITS):
                    act.wait_ge(cleared, u % 2 + 1)
                    if u >= 2:
                        act.wait_ge(rows_done, u - 1)
                    act.activation(pad[u % 2][:, PAD:PAD + IMG, PAD:PAD + IMG], m.X[:, u, :].rearrange("p (r c) -> p r c", c=IMG),
                                   ACT.Identity, bias=m.nbias[:, u:u + 1], scale=m.rstd[:, u:u + 1]).then_inc(padded, 1)

            @block.vector
            def _(dve):
                done = 0
                for u in range(UNITS):
                    img = m.X[:, u, :].rearrange("p (r c) -> p r c", c=IMG)
                    dve.wait_ge(padded, u + 1)
                    for a in range(KW):
                        for b in range(KW):
                            tap = (KW - 1 - a) * KW + KW - 1 - b
                            if done:
                                dve.wait_ge(tapped, done)
                            ins = dve.scalar_tensor_tensor(img, pad[u % 2][:, a:a + IMG, b:b + IMG], m.fir[:, tap:tap + 1], img, ALU.mult, ALU.add)
                            if (a, b) == (KW - 1, KW - 1):
                                ins.then_inc(rows_done, 1)
                            else:
                                ins.then_inc(tapped, 1)
                                done += 1
                dve.wait_ge(rows_done, UNITS)


def pipeline(eng, tiles, stages):
    def step(t, k, known):
        for fn, lag in stages:
            if not known or 0 <= k - lag < tiles:
                fn(eng, t - lag, (k - lag) % 2)
    lags = max(lag for _, lag in stages)
    head = lags + lags % 2
    for k in range(head):
        step(k, k, True)
    turns = (tiles - head) // 2
    with eng.Fori(0, turns) as i:
        for k in (head, head + 1):
            step(2 * i + k, k, False)
    for k in range(head + 2 * turns, tiles + lags):
        step(k, k, True)


def attention2(nc, m):
    with ExitStack() as outer:
        keep = lambda name, shape: outer.enter_context(nc.sbuf_tensor(name, shape, F32))
        gate_scale = keep("gate_scale", [P, UNITS])
        gate_bias = keep("gate_bias", [P, UNITS])
        channel_gate2(nc, m, gate_scale, gate_bias)
        for b in range(B):
            with ExitStack() as st:
                buf = lambda name, shape: st.enter_context(nc.sbuf_tensor(f"{name}_{b}", shape, F32))
                s = buf("gated", [P, HALVES, L])
                theta, phi, nl = buf("theta", [P, L]), buf("phi", [P, L]), buf("nl", [P, L])
                gT = buf("gT", [TILE, TILES, P])
                project2(nc, m, b, s, theta, phi, gT, gate_scale, gate_bias)
                softmax2(nc, m, b, theta, phi, gT, nl)
                project_out2(nc, m, b, s, nl)


def channel_gate2(nc, m, gate_scale, gate_bias):
    with ExitStack() as st:
        sb = lambda name: st.enter_context(nc.sbuf_tensor(name, [P, UNITS], F32))
        mean, scaled, std, z, ez, r2, z0 = (sb("cg_" + n) for n in ("mean", "scaled", "std", "z", "ez", "r2", "z0"))
        sem = st.enter_context(signals(nc, "gate"))
        chain, var_ready, std_ready, z_ready, exp_ready = (sem(n) for n in ("chain", "var_ready", "std_ready", "z_ready", "exp_ready"))

        def both(i):
            return m.cfc[:, :, i].unsqueeze(1).to_broadcast([P, B, HALVES])

        def units(t):
            return t[:, :].rearrange("p (b f) -> p b f", b=B)

        with nc.Block() as block:
            @block.vector
            def _(dve):
                done = [0]

                def link(ins):
                    done[0] += 1
                    ins.then_inc(chain, 1)
                    dve.wait_ge(chain, done[0])
                link(dve.tensor_tensor(mean[:, :], m.mv[:, :, 0], m.rstd[:, :], ALU.mult))
                link(dve.tensor_tensor(mean[:, :], mean[:, :], m.nbias[:, :], ALU.add))
                link(dve.tensor_tensor(r2[:, :], m.rstd[:, :], m.rstd[:, :], ALU.mult))
                link(dve.tensor_tensor(scaled[:, :], m.mv[:, :, 1], r2[:, :], ALU.mult))
                dve.tensor_scalar(scaled[:, :], scaled[:, :], float(L) / (L - 1), 1e-5, ALU.mult, ALU.add).then_inc(var_ready, 1)
                link(dve.tensor_tensor(units(z0), units(mean), both(0), ALU.mult))
                dve.wait_ge(std_ready, 1)
                link(dve.tensor_tensor(units(z), units(std), both(1), ALU.mult))
                dve.tensor_tensor(z[:, :], z[:, :], z0[:, :], ALU.add).then_inc(z_ready, 1)
                dve.wait_ge(exp_ready, 1)
                link(dve.tensor_scalar(ez[:, :], ez[:, :], 1.0, None, ALU.add))
                link(dve.reciprocal(z0[:, :], ez[:, :]))
                link(dve.tensor_tensor(gate_scale[:, :], m.rstd[:, :], z0[:, :], ALU.mult))
                link(dve.tensor_tensor(gate_bias[:, :], m.nbias[:, :], z0[:, :], ALU.mult))

            @block.scalar
            def _(act):
                act.wait_ge(var_ready, 1)
                act.activation(std[:, :], scaled[:, :], ACT.Sqrt).then_inc(std_ready, 1)
                act.wait_ge(z_ready, 1)
                act.activation(ez[:, :], z[:, :], ACT.Exp, scale=-1.0).then_inc(exp_ready, 1)


def project2(nc, m, b, s, theta, phi, gT, gate_scale, gate_bias):
    with ExitStack() as st:
        pp = [st.enter_context(nc.psum_tensor(f"pp{i}_{b}", [P, 512], F32)) for i in range(8)]
        sem = st.enter_context(signals(nc, f"p2_{b}"))
        gated, made, kept_a, kept_v = (sem(n) for n in ("gated", "made", "kept_a", "kept_v"))
        JOBS = 3 * CHUNKS
        with nc.Block() as block:
            @block.vector
            def _(dve):
                for f in range(HALVES):
                    u = HALVES * b + f
                    dve.tensor_scalar(s[:, f, :], m.X[:, u, :], gate_scale[:, u:u + 1], gate_bias[:, u:u + 1], ALU.mult, ALU.add).then_inc(gated, 1)
                for k in range(CHUNKS):
                    dve.wait_ge(made, 3 * k + 3)
                    dve.tensor_tensor(gT[:, 4 * k:4 * k + 4, :], pp[(3 * k + 2) % 8][0:TILE, :].rearrange("p (j c) -> p j c", j=4),
                                      m.gbias[0:TILE, :].unsqueeze(1).to_broadcast([TILE, 4, P]), ALU.add).then_inc(kept_v, 1)
                dve.wait_ge(kept_v, CHUNKS)

            @block.scalar
            def _(act):
                for k in range(CHUNKS):
                    for j, dst in enumerate((theta, phi)):
                        act.wait_ge(made, 3 * k + j + 1)
                        act.activation(dst[:, CHUNK * k:CHUNK * (k + 1)], pp[(3 * k + j) % 8][:, 0:CHUNK], ACT.Identity, bias=m.bias2[:, j:j + 1]).then_inc(kept_a, 1)
                act.wait_ge(kept_a, 2 * CHUNKS)

            @block.tensor
            def _(pe):
                pe.wait_ge(gated, HALVES)
                for n in range(JOBS):
                    k, j = n // 3, n % 3
                    if n >= 8:
                        kk, jj = (n - 8) // 3, (n - 8) % 3
                        if jj == 2:
                            pe.wait_ge(kept_v, kk + 1)
                        else:
                            pe.wait_ge(kept_a, 2 * kk + jj + 1)
                    bank = pp[n % 8]
                    if j < 2:
                        for i in range(HALVES):
                            mm = pe.matmul(bank[:, 0:CHUNK], m.WT[:, (W_THETA, W_PHI)[j] + i, :], s[:, i, CHUNK * k:CHUNK * (k + 1)],
                                           start=(i == 0), stop=(i == 1))
                    else:
                        for q in range(4):
                            at = TILE * (4 * k + q)
                            for i in range(HALVES):
                                mm = pe.matmul(bank[0:TILE, P * q:P * (q + 1)], s[:, i, at:at + TILE], m.WT[:, W_G + i, :],
                                               start=(i == 0), stop=(i == 1))
                    mm.then_inc(made, 1)


def softmax2(nc, m, b, theta, phi, gT, nl):
    SUB2 = L // 8
    with ExitStack() as st:
        sem = st.enter_context(signals(nc, f"a2_{b}"))
        sb = lambda name, shape: st.enter_context(nc.sbuf_tensor(f"a2_{name}_{b}", shape, F32))
        ps = lambda name, shape: st.enter_context(nc.psum_tensor(f"a2_{name}_{b}", shape, F32))
        q = [sb(f"q{r}", [P, TILE]) for r in range(2)]
        prob = [sb(f"prob{r}", [TILE, L]) for r in range(2)]
        probT = [sb(f"probT{r}", [TILE, 4, TILE]) for r in range(2)]
        o = [sb(f"o{r}", [TILE, P]) for r in range(2)]
        gmax = [sb(f"gmax{r}", [TILE, 4]) for r in range(2)]
        rmax = [sb(f"rmax{r}", [TILE, 1]) for r in range(2)]
        nmax = [sb(f"nmax{r}", [TILE, 1]) for r in range(2)]
        rsum = [sb(f"rsum{r}", [TILE, 1]) for r in range(2)]
        rinv = [sb(f"rinv{r}", [TILE, 1]) for r in range(2)]
        scp = [ps(f"scores{i}", [TILE, 2, 512]) for i in range(2)]
        tp = [ps(f"turned{i}", [TILE, 4, TILE]) for i in range(2)]
        op = ps("op", [TILE, P])
        otp = ps("otp", [P, TILE])
        q_ready, s_made, s_copied, max_step, max_ready, exp_done, turned, copied_v, copied_a, pv_done, inv_ready, o_normed, o_turned, o_placed = (
            sem(n) for n in ("q_ready", "s_made", "s_copied", "max_step", "max_ready", "exp_done", "turned", "copied_v", "copied_a", "pv_done", "inv_ready", "o_normed", "o_turned", "o_placed"))

        def copied(c, t):
            return (copied_v, 4 * (t + 1) + c // 2 + 1) if c % 2 == 0 else (copied_a, 3 * (t + 1) + c // 2 + 1)

        def copy_chunk(eng, copy, t, r, c, done):
            eng.wait_ge(turned, 7 * t + c + 1 + 14)
            if c >= 2:
                eng.wait_ge(pv_done, 7 * (t + 1) + c - 1)
            else:
                eng.wait_ge(pv_done, 7 * t + 6 + c)
            copy(probT[(r + c) % 2][:, :, :], tp[(r + c) % 2][:, :, :]).then_inc(done, 1)

        with nc.Block() as block:
            @block.gpsimd
            def _(pool):
                def stage_q(eng, t, r):
                    eng.wait_ge(s_made, 4 * (t + 1))
                    eng.tensor_copy(q[r][:, :], theta[:, bass.ds(TILE * t, TILE)]).then_inc(q_ready, 1)
                pipeline(pool, TILES, [(stage_q, 0)])

            @block.tensor
            def _(pe):
                def scores(eng, t, r):
                    eng.wait_ge(q_ready, t + 1)
                    for g in range(4):
                        eng.wait_ge(s_copied, 4 * t + g + 1)
                        for j in range(2):
                            at = SUB2 * (2 * g + j)
                            mm = eng.matmul(scp[g % 2][:, j, 0:SUB2], q[r][:, :], phi[:, at:at + SUB2], start=True, stop=True)
                        mm.then_inc(s_made, 1)

                def values(eng, t, r):
                    eng.wait_ge(exp_done, t + 1)
                    for c in range(CHUNKS + 1):
                        if c < CHUNKS:
                            eng.wait_ge(*(copied(c - 2, t) if c >= 2 else copied(c + 5, t - 1)))
                            for j in range(4):
                                at = TILE * (4 * c + j)
                                mm = eng.transpose(tp[(r + c) % 2][:, j, :], prob[r][:, at:at + TILE], m.ident[0:TILE, 0:TILE])
                            mm.then_inc(turned, 1)
                        if c == 1:
                            eng.wait_ge(o_normed, t + 1)
                        if c >= 1:
                            eng.wait_ge(*copied(c - 1, t))
                            for j in range(4):
                                k = 4 * (c - 1) + j
                                mm = eng.matmul(op[:, :], probT[(r + c - 1) % 2][:, j, :], gT[:, k, :], start=(k == 0), stop=(k == TILES - 1))
                            mm.then_inc(pv_done, 1)

                def turn_out(eng, t, r):
                    eng.wait_ge(o_normed, t + 2)
                    eng.wait_ge(o_placed, t + 1)
                    eng.transpose(otp[:, :], o[r][:, :], m.ident[0:TILE, 0:TILE]).then_inc(o_turned, 1)

                pe.sem_inc(s_made, 8)
                pe.sem_inc(turned, 14)
                pe.sem_inc(pv_done, 7)
                pe.sem_inc(o_turned, 2)
                pipeline(pe, TILES, [(scores, 0), (turn_out, 2), (values, 1)])

            @block.vector
            def _(dve):
                def row_max(eng, t, r):
                    eng.wait_ge(turned, 7 * (t + 1))
                    for g in range(4):
                        eng.wait_ge(s_made, 4 * t + g + 9)
                        eng.tensor_scalar(prob[r][:, 2 * SUB2 * g:2 * SUB2 * (g + 1)].rearrange("p (j c) -> p j c", j=2), scp[g % 2][:, :, 0:SUB2],
                                          1.0, None, ALU.mult, ALU.max, accum_out=gmax[r][:, g:g + 1]).then_inc(s_copied, 1)
                    eng.wait_ge(s_copied, 4 * t + 6)
                    eng.tensor_reduce(rmax[r][:, :], gmax[r][:, :], AX.X, ALU.max).then_inc(max_step, 1)
                    eng.wait_ge(max_step, t + 1)
                    eng.tensor_scalar(nmax[r][:, :], rmax[r][:, :], -1.0, None, ALU.mult).then_inc(max_ready, 1)

                def normalise(eng, t, r):
                    for c in (0, 2, 4, 6):
                        copy_chunk(eng, eng.tensor_copy, t, r, c, copied_v)
                    eng.reciprocal(rinv[r][:, :], rsum[r][:, :]).then_inc(inv_ready, 1)
                    eng.wait_ge(inv_ready, t + 1)
                    eng.wait_ge(pv_done, 7 * (t + 2))
                    eng.wait_ge(o_turned, t + 1)
                    eng.tensor_scalar(o[r][:, :], op[:, :], rinv[r][:, :], None, ALU.mult).then_inc(o_normed, 1)

                dve.sem_inc(s_copied, 2)
                dve.sem_inc(copied_v, 4)
                dve.sem_inc(o_normed, 1)
                pipeline(dve, TILES, [(row_max, 0), (normalise, 1)])

            @block.scalar
            def _(act):
                def copies(eng, t, r):
                    for c in (1, 3, 5):
                        copy_chunk(eng, eng.copy, t, r, c, copied_a)

                def place_out(eng, t, r):
                    eng.wait_ge(o_turned, t + 3)
                    eng.copy(nl[:, bass.ds(TILE * t, TILE)], otp[:, :]).then_inc(o_placed, 1)

                def exponent(eng, t, r):
                    eng.wait_ge(max_ready, t + 1)
                    eng.activation(prob[r][:, :], prob[r][:, :], ACT.Exp, bias=nmax[r][:, :], accum_out=rsum[r][:, :]).then_inc(exp_done, 1)

                act.sem_inc(copied_a, 3)
                act.sem_inc(o_placed, 1)
                pipeline(act, TILES, [(copies, 1), (place_out, 2), (exponent, 0)])
                act.wait_ge(o_placed, TILES + 1)


def project_out2(nc, m, b, s, nl):
    with ExitStack() as st:
        yp = [st.enter_context(nc.psum_tensor(f"y2p{i}_{b}", [P, 512], F32)) for i in range(8)]
        sem = st.enter_context(signals(nc, f"y2_{b}"))
        made, added, with_s = (sem(n) for n in ("made", "added", "with_s"))
        with nc.Block() as block:
            @block.tensor
            def _(pe):
                for n in range(HALVES * CHUNKS):
                    f, k = n // CHUNKS, n % CHUNKS
                    if n >= 8:
                        pe.wait_ge(added, n - 7)
                    pe.matmul(yp[n % 8][:, 0:CHUNK], m.WT[:, W_OUT + f, :], nl[:, CHUNK * k:CHUNK * (k + 1)], start=True, stop=True).then_inc(made, 1)

            @block.vector
            def _(dve):
                for f in range(HALVES):
                    X = m.X[:, HALVES * b + f, :]
                    dve.tensor_tensor(X, X, s[:, f, :], ALU.add).then_inc(with_s, 1)
                for n in range(HALVES * CHUNKS):
                    f, k = n // CHUNKS, n % CHUNKS
                    dve.wait_ge(made, n + 1)
                    dve.wait_ge(with_s, f + 1)
                    X = m.X[:, HALVES * b + f, CHUNK * k:CHUNK * (k + 1)]
                    dve.scalar_tensor_tensor(X, yp[n % 8][:, 0:CHUNK], m.bias2[:, 2 + f:3 + f], X, ALU.add, ALU.add).then_inc(added, 1)
                dve.wait_ge(added, HALVES * CHUNKS)


def attention3(nc, m):
    with ExitStack() as outer:
        keep = lambda name, shape: outer.enter_context(nc.sbuf_tensor(name, shape, F32))
        c = keep("spline_c", [P, 8])
        half_base = keep("half_base", [P, 1])
        linear = keep("linear", [P, 1])
        spline_constants3(nc, m, c, half_base, linear)
        for b in range(B):
            with ExitStack() as st:
                buf = lambda name, shape: st.enter_context(nc.sbuf_tensor(f"{name}_{b}", shape, F32))
                Q, K, O = buf("Q3", [P, L]), buf("K3", [P, L]), buf("O3", [P, L])
                V = buf("V3", [TILE, TILES, P])
                project3(nc, m, b, Q, K, V)
                for pair in range(2):
                    kan_attention3(nc, m, b, pair, Q, K, V, O, c, half_base, linear)
                project_out3(nc, m, b, O)


def spline_constants3(nc, m, c, half_base, linear):
    with ExitStack() as st:
        prod = st.enter_context(nc.sbuf_tensor("sc_prod", [P, 8, 8], F32))
        scaled = st.enter_context(nc.sbuf_tensor("sc_scaled", [P, 8], F32))
        chain = st.enter_context(signals(nc, "sc"))("chain")
        with nc.Block() as block:
            @block.vector
            def _(dve):
                done = [0]

                def link(ins):
                    done[0] += 1
                    ins.then_inc(chain, 1)
                    dve.wait_ge(chain, done[0])
                link(dve.tensor_scalar(scaled[:, :], m.coef[:, :], m.scaler[:, :], None, ALU.mult))
                link(dve.tensor_tensor(prod[:, :, :], m.smat[:, :, :], scaled[:, :].unsqueeze(1).to_broadcast([P, 8, 8]), ALU.mult))
                link(dve.tensor_reduce(c[:, :], prod[:, :, :], AX.X, ALU.add))
                link(dve.tensor_scalar(half_base[:, :], m.basew[:, :], 0.5, None, ALU.mult))
                link(dve.tensor_tensor(linear[:, :], c[:, 2:3], half_base[:, :], ALU.add))


def project3(nc, m, b, Q, K, V):
    scale = 1.0 / float(np.sqrt(HD3))
    with ExitStack() as st:
        xn = st.enter_context(nc.sbuf_tensor(f"xn3_{b}", [P, HALVES, L], F32))
        pp = [st.enter_context(nc.psum_tensor(f"p3p{i}_{b}", [P, 512], F32)) for i in range(8)]
        sem = st.enter_context(signals(nc, f"p3_{b}"))
        normed, made, kept_a, kept_v = (sem(n) for n in ("normed", "made", "kept_a", "kept_v"))
        JOBS = 3 * CHUNKS
        with nc.Block() as block:
            @block.vector
            def _(dve):
                for f in range(HALVES):
                    u = HALVES * b + f
                    dve.tensor_scalar(xn[:, f, :], m.X[:, u, :], m.rstd[:, u:u + 1], m.nbias[:, u:u + 1], ALU.mult, ALU.add).then_inc(normed, 1)
                for k in range(CHUNKS):
                    dve.wait_ge(made, 3 * k + 3)
                    dve.tensor_copy(V[:, 4 * k:4 * k + 4, :], pp[(3 * k + 2) % 8][0:TILE, :].rearrange("p (j c) -> p j c", j=4)).then_inc(kept_v, 1)
                dve.wait_ge(kept_v, CHUNKS)

            @block.scalar
            def _(act):
                for k in range(CHUNKS):
                    for j, dst in enumerate((Q, K)):
                        act.wait_ge(made, 3 * k + j + 1)
                        act.activation(dst[:, CHUNK * k:CHUNK * (k + 1)], pp[(3 * k + j) % 8][:, 0:CHUNK], ACT.Copy, scale=(scale, 1.0)[j]).then_inc(kept_a, 1)
                act.wait_ge(kept_a, 2 * CHUNKS)

            @block.tensor
            def _(pe):
                pe.wait_ge(normed, HALVES)
                for n in range(JOBS):
                    k, j = n // 3, n % 3
                    if n >= 8:
                        kk, jj = (n - 8) // 3, (n - 8) % 3
                        if jj == 2:
                            pe.wait_ge(kept_v, kk + 1)
                        else:
                            pe.wait_ge(kept_a, 2 * kk + jj + 1)
                    bank = pp[n % 8]
                    if j < 2:
                        for i in range(HALVES):
                            mm = pe.matmul(bank[:, 0:CHUNK], m.WT[:, (W_Q3, W_K3)[j] + i, :], xn[:, i, CHUNK * k:CHUNK * (k + 1)],
                                           start=(i == 0), stop=(i == 1))
                    else:
                        for q in range(4):
                            at = TILE * (4 * k + q)
                            for i in range(HALVES):
                                mm = pe.matmul(bank[0:TILE, P * q:P * (q + 1)], xn[:, i, at:at + TILE], m.WT[:, W_V3 + i, :],
                                               start=(i == 0), stop=(i == 1))
                    mm.then_inc(made, 1)


def kan_attention3(nc, m, b, pair, Q, K, V, O, c, half_base, linear):
    QUART = L // 4
    rows = slice(2 * HD3 * pair, 2 * HD3 * (pair + 1))
    with ExitStack() as st:
        tag = f"{b}{pair}"
        sem = st.enter_context(signals(nc, "a3_" + tag))
        sb = lambda name, shape: st.enter_context(nc.sbuf_tensor(f"a3_{name}_{tag}", shape, F32))
        ps = lambda name, shape: st.enter_context(nc.psum_tensor(f"a3_{name}_{tag}", shape, F32))
        q = [sb(f"q{r}", [P, P]) for r in range(2)]
        prob = [sb(f"prob{r}", [P, L]) for r in range(2)]
        probT = [sb(f"probT{r}", [TILE, 4, P]) for r in range(2)]
        x = [sb(f"x{g}", [P, QUART]) for g in range(4)]
        th = [sb(f"th{g}", [P, QUART]) for g in range(2)]
        v1 = [sb(f"v1{g}", [P, QUART]) for g in range(2)]
        v2 = [sb(f"v2{g}", [P, QUART]) for g in range(2)]
        s1 = [sb(f"s1{g}", [P, QUART]) for g in range(2)]
        s2 = [sb(f"s2{g}", [P, QUART]) for g in range(2)]
        right = [sb(f"right{g}", [P, QUART]) for g in range(2)]
        knots = sb("knots", [P, 2])
        o = [sb(f"o{r}", [P, HD3]) for r in range(2)]
        gmax = [sb(f"gmax{r}", [P, 4]) for r in range(2)]
        rmax = [sb(f"rmax{r}", [P, 1]) for r in range(2)]
        nmax = [sb(f"nmax{r}", [P, 1]) for r in range(2)]
        rsum = [sb(f"rsum{r}", [P, 1]) for r in range(2)]
        rinv = [sb(f"rinv{r}", [P, 1]) for r in range(2)]
        scp = [ps(f"scores{i}", [P, 2, 512]) for i in range(2)]
        tp = [ps(f"turned{i}", [TILE, 4, P]) for i in range(2)]
        op = ps("op", [P, 2 * HD3])
        otp = ps("otp", [HD3, P])
        (q_ready, q_zeroed, knots_set, s_made, clipped, tanh_ready, v_ready, s_ready, cubed, right_step, right_ready,
         poly_step, based, left_added, right_gated, all_added, max_step, max_ready, exp_done, turned, copied, pv_done,
         inv_ready, o_normed, o_turned, o_placed, waits_met_v, waits_met_p) = (
            sem(n) for n in ("q_ready", "q_zeroed", "knots_set", "s_made", "clipped", "tanh_ready", "v_ready", "s_ready", "cubed",
                             "right_step", "right_ready", "poly_step", "based", "left_added", "right_gated", "all_added",
                             "max_step", "max_ready", "exp_done", "turned", "copied", "pv_done", "inv_ready", "o_normed",
                             "o_turned", "o_placed", "waits_met_v", "waits_met_p"))

        with nc.Block() as block:
            @block.gpsimd
            def _(pool):
                def stage_q(eng, t, r):
                    eng.wait_ge(s_made, 4 * (t + 1))
                    eng.wait_ge(right_ready, 4 * t + 4)
                    for h in range(2):
                        hrows = slice(HD3 * (2 * pair + h), HD3 * (2 * pair + h + 1))
                        if h:
                            eng.wait_ge(q_ready, 2 * t + 1)
                        eng.tensor_copy(q[r][hrows, QT3 * h:QT3 * (h + 1)], Q[hrows, bass.ds(QT3 * t, QT3)]).then_inc(q_ready, 1)
                    eng.wait_ge(q_ready, 2 * t + 2)

                def cubes(g):
                    def stage(eng, t, r):
                        n, G = 4 * t + g, g % 2
                        eng.wait_ge(s_ready, 2 * n + 1)
                        eng.tensor_tensor(v1[G][:, :], v1[G][:, :], s1[G][:, :], ALU.mult).then_inc(cubed, 1)
                        eng.wait_ge(s_ready, 2 * n + 2)
                        eng.tensor_tensor(v2[G][:, :], v2[G][:, :], s2[G][:, :], ALU.mult).then_inc(cubed, 1)
                        eng.wait_ge(cubed, 2 * n + 2)
                        eng.wait_ge(all_added, n + 1)
                        eng.sem_inc(waits_met_p, 1)
                        eng.tensor_scalar(right[G][:, :], v1[G][:, :], c[:, 5:6], 1.0, ALU.mult, ALU.mult).then_inc(right_step, 1)
                        eng.tensor_scalar(s2[G][:, :], v2[G][:, :], c[:, 6:7], 1.0, ALU.mult, ALU.mult).then_inc(right_step, 1)
                        eng.wait_ge(right_step, 2 * n + 2)
                        eng.tensor_tensor(right[G][:, :], right[G][:, :], s2[G][:, :], ALU.add).then_inc(right_ready, 1)
                    return stage

                for r in range(2):
                    pool.memset(q[r][rows, :], 0.0).then_inc(q_zeroed, 1)
                pool.wait_ge(q_zeroed, 2)
                for j, t in enumerate((KNOT_IN, KNOT_OUT)):
                    pool.memset(knots[:, j:j + 1], -t).then_inc(knots_set, 1)
                    pool.wait_ge(knots_set, j + 1)
                pool.sem_inc(right_ready, 6)
                pipeline(pool, TILES3, [(stage_q, 0), (cubes(2), 1), (cubes(3), 1), (cubes(0), 0), (cubes(1), 0)])

            @block.tensor
            def _(pe):
                def scores(g):
                    def stage(eng, t, r):
                        if g == 0:
                            eng.wait_ge(q_ready, 2 * (t + 1))
                        eng.wait_ge(clipped, 4 * t + g + 1)
                        for j in range(2):
                            at = SUB * (2 * g + j)
                            mm = eng.matmul(scp[g % 2][:, j, 0:SUB], q[r][rows, :], K[rows, at:at + SUB], start=True, stop=True)
                        mm.then_inc(s_made, 1)
                    return stage

                def values(eng, t, r):
                    eng.wait_ge(exp_done, t + 1)
                    for ch in range(CHUNKS + 1):
                        if ch < CHUNKS:
                            eng.wait_ge(copied, 7 * t + ch + 1)
                            for j in range(4):
                                at = TILE * (4 * ch + j)
                                mm = eng.transpose(tp[(r + ch) % 2][:, j, :], prob[r][:, at:at + TILE], m.ident[:, :])
                            mm.then_inc(turned, 1)
                        if ch == 1:
                            eng.wait_ge(o_normed, 2 * (t + 1))
                        if ch >= 1:
                            eng.wait_ge(copied, 7 * t + ch + 2)
                            for j in range(4):
                                k = 4 * (ch - 1) + j
                                mm = eng.matmul(op[:, :], probT[(r + ch - 1) % 2][:, j, :], V[:, k, rows], start=(k == 0), stop=(k == TILES - 1))
                            mm.then_inc(pv_done, 1)

                def turn_out(eng, t, r):
                    eng.wait_ge(o_normed, 2 * (t + 2))
                    eng.wait_ge(o_placed, 2 * (t + 1))
                    eng.transpose(otp[:, :], o[r][:, :], m.ident[:, :]).then_inc(o_turned, 1)

                pe.sem_inc(s_made, 8)
                pe.sem_inc(turned, 14)
                pe.sem_inc(pv_done, 7)
                pe.sem_inc(o_turned, 2)
                pipeline(pe, TILES3, [(scores(0), 0), (scores(1), 0), (values, 2), (scores(2), 0), (scores(3), 0), (turn_out, 3)])

            @block.vector
            def _(dve):
                def clip(g):
                    def stage(eng, t, r):
                        eng.wait_ge(s_made, 4 * t + g + 9)
                        eng.tensor_scalar(x[g][:, :].rearrange("p (j c) -> p j c", j=2), scp[g % 2][:, :, 0:SUB], 6.0, -6.0, ALU.min, ALU.max).then_inc(clipped, 1)
                    return stage

                def base(g, part):
                    def stage(eng, t, r):
                        n, X, f = 4 * t + g, x[g][:, :], prob[r][:, QUART * g:QUART * (g + 1)]
                        if part == 0:
                            if g == 0:
                                eng.wait_ge(turned, 7 * (t + 1))
                            eng.wait_ge(clipped, n + 3)
                            eng.tensor_scalar(f, X, c[:, 0:1], c[:, 1:2], ALU.mult, ALU.add).then_inc(poly_step, 1)
                        elif part == 1:
                            eng.wait_ge(poly_step, 3 * n + 1)
                            eng.tensor_tensor(f, f, X, ALU.mult).then_inc(poly_step, 1)
                        elif part == 2:
                            eng.wait_ge(tanh_ready, n + 1)
                            eng.wait_ge(poly_step, 3 * n + 2)
                            eng.scalar_tensor_tensor(f, th[g % 2][:, :], half_base[:, :], f, ALU.mult, ALU.add).then_inc(poly_step, 1)
                        else:
                            eng.wait_ge(poly_step, 3 * n + 3)
                            eng.scalar_tensor_tensor(f, f, linear[:, :], X, ALU.add, ALU.mult).then_inc(based, 1)
                    return stage

                def left(g, part):
                    def stage(eng, t, r):
                        n, f = 4 * t + g, prob[r][:, QUART * g:QUART * (g + 1)]
                        eng.wait_ge(cubed, 2 * n + part + 1)
                        if part == 0:
                            eng.wait_ge(based, n + 3)
                        else:
                            eng.wait_ge(left_added, 2 * n + 5)
                        v = (v1, v2)[part][g % 2]
                        eng.scalar_tensor_tensor(f, v[:, :], c[:, 3 + part:4 + part], f, ALU.mult, ALU.add).then_inc(left_added, 1)
                    return stage

                def gate(g):
                    def stage(eng, t, r):
                        R = right[g % 2][:, :]
                        eng.wait_ge(right_ready, 4 * t + g + 7)
                        eng.scalar_tensor_tensor(R, x[g][:, :], 0.0, R, ALU.is_gt, ALU.mult).then_inc(right_gated, 1)
                    return stage

                def add_right(g):
                    def stage(eng, t, r):
                        n, f = 4 * t + g, prob[r][:, QUART * g:QUART * (g + 1)]
                        eng.wait_ge(right_gated, n + 1)
                        eng.wait_ge(left_added, 2 * n + 6)
                        eng.sem_inc(waits_met_v, 1)
                        eng.tensor_tensor_reduce(out=f, in0=f, in1=right[g % 2][:, :], scale=1.0, scalar=-3.0e38, op0=ALU.add, op1=ALU.max,
                                                 accum_out=gmax[r][:, g:g + 1]).then_inc(all_added, 1)
                    return stage

                def row_max(eng, t, r):
                    eng.wait_ge(all_added, 4 * t + 6)
                    eng.tensor_reduce(rmax[r][:, :], gmax[r][:, :], AX.X, ALU.max).then_inc(max_step, 1)
                    eng.wait_ge(max_step, t + 1)
                    eng.tensor_scalar(nmax[r][:, :], rmax[r][:, :], -1.0, None, ALU.mult).then_inc(max_ready, 1)

                def normalise(eng, t, r):
                    eng.wait_ge(exp_done, t + 1)
                    eng.reciprocal(rinv[r][:, :], rsum[r][:, :]).then_inc(inv_ready, 1)
                    eng.wait_ge(inv_ready, t + 1)
                    eng.wait_ge(pv_done, 7 * (t + 2))
                    eng.wait_ge(o_turned, t + 1)
                    for h in range(2):
                        qrows = slice(QT3 * h, QT3 * (h + 1))
                        eng.tensor_scalar(o[r][qrows, :], op[qrows, HD3 * h:HD3 * (h + 1)], rinv[r][qrows, :], None, ALU.mult).then_inc(o_normed, 1)

                dve.sem_inc(clipped, 2)
                dve.sem_inc(based, 2)
                dve.sem_inc(left_added, 4)
                dve.sem_inc(all_added, 2)
                dve.sem_inc(o_normed, 2)
                order = []
                for g in range(4):
                    b1, b2, b3 = ((g - back) % 4 for back in (1, 2, 3))
                    l1, l2, l3 = (int(g < back) for back in (1, 2, 3))
                    order += [(clip(g), 0), (left(b2, 0), l2), (base(b1, 0), l1), (left(b2, 1), l2), (base(b1, 1), l1),
                              (gate(b3), l3), (base(b1, 2), l1), (add_right(b3), l3), (base(b1, 3), l1)]
                    if g == 1:
                        order.append((normalise, 2))
                    if g == 2:
                        order.append((row_max, 1))
                pipeline(dve, TILES3, order)

            @block.scalar
            def _(act):
                def plane(g, which):
                    def stage(eng, t, r):
                        n, G = 4 * t + g, g % 2
                        if which == "tanh":
                            eng.wait_ge(clipped, n + 3)
                            eng.wait_ge(based, n + 1)
                            eng.activation(th[G][:, :], x[g][:, :], ACT.Tanh, scale=0.5).then_inc(tanh_ready, 1)
                        elif which == "abs":
                            eng.wait_ge(left_added, 2 * n + 2)
                            eng.wait_ge(right_ready, n + 5)
                            eng.activation(v2[G][:, :], x[g][:, :], ACT.Abs).then_inc(v_ready, 1)
                        elif which == "v1":
                            eng.wait_ge(v_ready, 3 * n + 1)
                            eng.activation(v1[G][:, :], v2[G][:, :], ACT.Relu, bias=knots[:, 0:1]).then_inc(v_ready, 1)
                        elif which == "v2":
                            eng.wait_ge(v_ready, 3 * n + 2)
                            eng.activation(v2[G][:, :], v2[G][:, :], ACT.Relu, bias=knots[:, 1:2]).then_inc(v_ready, 1)
                        elif which == "s1":
                            eng.wait_ge(v_ready, 3 * n + 2)
                            eng.activation(s1[G][:, :], v1[G][:, :], ACT.Square).then_inc(s_ready, 1)
                        else:
                            eng.wait_ge(v_ready, 3 * n + 3)
                            eng.activation(s2[G][:, :], v2[G][:, :], ACT.Square).then_inc(s_ready, 1)
                    return stage

                def copies(ch):
                    def stage(eng, t, r):
                        eng.wait_ge(turned, 7 * t + ch + 15)
                        eng.wait_ge(pv_done, 7 * (t + 1) + ch - 1)
                        eng.copy(probT[(r + ch) % 2][:, :, :], tp[(r + ch) % 2][:, :, :]).then_inc(copied, 1)
                    return stage

                def place_out(eng, t, r):
                    eng.wait_ge(o_turned, t + 3)
                    for h in range(2):
                        hrows = slice(HD3 * (2 * pair + h), HD3 * (2 * pair + h + 1))
                        eng.copy(O[hrows, bass.ds(QT3 * t, QT3)], otp[:, QT3 * h:QT3 * (h + 1)]).then_inc(o_placed, 1)

                def exponent(eng, t, r):
                    eng.wait_ge(max_ready, t + 1)
                    eng.activation(prob[r][:, :], prob[r][:, :], ACT.Exp, bias=nmax[r][:, :], accum_out=rsum[r][:, :]).then_inc(exp_done, 1)

                act.wait_ge(knots_set, 2)
                act.sem_inc(copied, 2)
                act.sem_inc(o_placed, 2)
                planes = ("tanh", "abs", "v1", "s1", "v2", "s2")
                order = [(plane(0, "tanh"), 0), (copies(5), 2), (plane(0, "abs"), 0), (copies(6), 2)]
                order += [(plane(0, w), 0) for w in planes[2:]] + [(place_out, 3)]
                order += [(plane(g, w), 0) for g in (1, 2) for w in planes] + [(exponent, 1)]
                order += [(plane(3, w), 0) for w in planes[:2]]
                for ch in range(5):
                    order.append((copies(ch), 1))
                    if ch < 4:
                        order.append((plane(3, planes[2 + ch]), 0))
                pipeline(act, TILES3, order)
                act.wait_ge(o_placed, 2 * (TILES3 + 1))


def project_out3(nc, m, b, O):
    with ExitStack() as st:
        yp = [st.enter_context(nc.psum_tensor(f"y3p{i}_{b}", [P, 512], F32)) for i in range(8)]
        sem = st.enter_context(signals(nc, f"y3_{b}"))
        made, added = (sem(n) for n in ("made", "added"))
        with nc.Block() as block:
            @block.tensor
            def _(pe):
                for n in range(HALVES * CHUNKS):
                    f, k = n // CHUNKS, n % CHUNKS
                    if n >= 8:
                        pe.wait_ge(added, n - 7)
                    pe.matmul(yp[n % 8][:, 0:CHUNK], m.WT[:, W_O3 + f, :], O[:, CHUNK * k:CHUNK * (k + 1)], start=True, stop=True).then_inc(made, 1)

            @block.vector
            def _(dve):
                for n in range(HALVES * CHUNKS):
                    f, k = n // CHUNKS, n % CHUNKS
                    dve.wait_ge(made, n + 1)
                    X = m.X[:, HALVES * b + f, CHUNK * k:CHUNK * (k + 1)]
                    dve.tensor_tensor(X, X, yp[n % 8][:, 0:CHUNK], ALU.add).then_inc(added, 1)
                dve.wait_ge(added, HALVES * CHUNKS)


_INS = ["x", "L0_conv_qkv_w", "L0_conv_qkv_b", "L0_conv_proj_w", "L0_conv_proj_b", "L0_conv_relative_bias", "L1_conv_kernel",
        "L2_conv_cfc", "L2_conv_theta_w", "L2_conv_theta_b", "L2_conv_phi_w", "L2_conv_phi_b", "L2_conv_g_w", "L2_conv_g_b",
        "L2_conv_out_w", "L2_conv_out_b", "L3_conv_Wq", "L3_conv_Wk", "L3_conv_Wv", "L3_conv_Wo", "L3_conv_base_w",
        "L3_conv_spline_w", "L3_conv_spline_scaler"]


def kernel(**inputs):
    import numpy as _np
    import concourse.bacc as _bacc
    from concourse import mybir as _mybir
    from concourse.bass_utils import run_bass_kernel_spmd as _run

    nc = _bacc.Bacc("TRN2", target_bir_lowering=False, num_devices=1)
    arrays, args = {}, []
    values = [(name, inputs[name]) for name in _INS] + [("window_mask", window_mask()), ("spline_matrix", spline_matrix())]
    for name, value in values:
        a = _np.ascontiguousarray(value)
        arrays[f"in_{name}_dram"] = a
        args.append(nc.dram_tensor(f"in_{name}_dram", a.shape, _mybir.dt.from_np(a.dtype), kind="ExternalInput").ap())
    args.append(nc.dram_tensor("out_0_dram", (B, HALVES * P, IMG, IMG), F32, kind="ExternalOutput").ap())
    conv_preact_kernel(nc, *args)
    r = _run(nc, [arrays], core_ids=[0])
    return r.results[0]["out_0_dram"]
```

```python
from contextlib import ExitStack, contextmanager

import numpy as np

import concourse.bass as bass
from concourse import mybir

F32 = mybir.dt.float32
ALU = mybir.AluOpType
ACT = mybir.ActivationFunctionType
AX = mybir.AxisListType

P = 128
B = 2
HALVES = 2
UNITS = B * HALVES
IMG = 56
L = IMG * IMG
CHUNK = 8 * IMG
CHUNKS = L // CHUNK
GN_EPS = 1e-5

WS = 7
GRID = IMG - WS + 1
KEYS = WS * WS
HEADS0 = 8
HD0 = 32
TILE = 2 * IMG
TILES = L // TILE
DY_STEP = 356
DX_STEP = 51
WIN = 4
COLS = (WS + 1) * WS * WIN
EXTRA = WS * DY_STEP
BOTTOM_SHIFT = 8
PAIR0 = 2860
CORNER0 = PAIR0 + 6 * 51
QCOLS = CORNER0 + 4 * 12
PAIR_W = 104
ONEHOT_OFF = 147
BIAS_ROWS = GRID + IMG + 2 * (TILES - 1)
ONEHOT_W = ONEHOT_OFF + BIAS_ROWS + 36
BIAS_ROW = (WS * WIN + 6 * WIN) * HEADS0
CORNER_PIX = (0, 48 * IMG + 1, 7 * IMG + 6, 55 * IMG + 7)

HEADS3 = 4
HD3 = 32
QT3 = 64
TILES3 = L // QT3
HALF = L // 2
SUB = HALF // 4
KNOT_H = 2.4
KNOT_IN, KNOT_OUT = 1.2, 3.6

W_QKV, W_PROJ, W_THETA, W_PHI, W_G, W_OUT, W_Q3, W_K3, W_V3, W_O3, W_BLOCKS = \
    0, 12, 16, 18, 20, 22, 24, 26, 28, 30, 32


def spline_matrix():
    h = KNOT_H
    m = np.zeros((8, 8))
    u3, u2, u1, one = [np.array(v) for v in ((1.0, 1.5, 0.75, 0.125), (0, 1.0, 1.0, 0.25), (0, 0, 1.0, 0.5), (0, 0, 0, 1.0))]
    pieces = {5: u3, 4: -3 * u3 + 3 * u2 + 3 * u1 + one, 3: 3 * u3 - 6 * u2 + 4 * one, 2: -u3 + 3 * u2 - 3 * u1 + one}
    for k, p in pieces.items():
        for row, power in ((0, 3), (1, 2), (2, 1), (7, 0)):
            m[row, k] = p[3 - power] / 6 / h ** power
    binom = (1, 4, 6, 4, 1)
    for j in range(5):
        c = (-1) ** j * binom[j] / (6 * h ** 3)
        m[3, j + 1] += c
        m[4, j] += c
        m[5, 6 - j] += c
        m[6, 7 - j] += c
    m[5] -= m[3]
    m[6] -= m[4]
    return m.astype(np.float32)


def window_mask():
    m = np.zeros((TILES, TILE, WS + 1, WS, WIN), np.float32)
    p = np.arange(TILE)
    col = p % IMG
    for t in range(TILES):
        row = 2 * t + p // IMG
        for w in range(WIN):
            place = 2 * t + 50 * (p // IMG) + col - KEYS * w
            for dx in range(WS):
                for dy in range(WS):
                    j = place + 6 * dy
                    m[t, :, dy, dx, w] = (j >= 0) & (j < KEYS) & (col >= dx) & (col < dx + GRID) & (row >= dy) & (row < dy + GRID)
                if 1 <= dx <= 3:
                    m[t, :, WS, dx, w] = (place >= 0) & (place < KEYS) & (col < GRID) & (row < GRID - 1)
                if dx > 3:
                    j = place + 36
                    m[t, :, WS, dx, w] = (j >= 0) & (j < KEYS) & (col >= WS - 1) & (row >= WS)
    return m.reshape(TILES, TILE, COLS)




@contextmanager
def signals(nc, tag):
    with ExitStack() as st:
        made = []

        def make(name):
            made.append(st.enter_context(nc.semaphore(f"{name}_{tag}")))
            return made[-1]
        yield make
        with nc.Block() as block:
            @block.sync
            def _(sp):
                for s in made:
                    sp.sem_clear(s)
class OnChip:
    pass


def conv_preact_kernel(nc, x, qkv_w, qkv_b, proj_w, proj_b, rel_bias, fir, cfc, theta_w, theta_b,
                       phi_w, phi_b, g_w, g_b, out_w, out_b, wq3, wk3, wv3, wo3, base_w, spline_w,
                       spline_scaler, mask_dram, spline_m, out):
    with ExitStack() as ctx:
        def sb(name, shape):
            return ctx.enter_context(nc.sbuf_tensor(name, shape, F32))

        m = OnChip()
        m.X = sb("X", [P, UNITS, L])
        m.WT = sb("WT", [P, W_BLOCKS, P])
        m.ident = sb("ident", [P, P])
        m.group = sb("group", [P, P])
        m.rstd = sb("rstd", [P, UNITS])
        m.nbias = sb("nbias", [P, UNITS])
        m.mv = sb("mv", [P, UNITS, 2])
        m.qkvb = sb("qkvb", [P, 6])
        m.pbias = sb("pbias", [P, HALVES])
        m.vbias = sb("vbias", [P, HALVES * P])
        m.rb = sb("rb", [KEYS, WS, WS, HEADS0])
        m.fir = sb("fir_taps", [P, 16])
        m.cfc = sb("cfc", [P, HALVES, 2])
        m.bias2 = sb("bias2", [P, 4])
        m.gbias = sb("gbias", [P, P])
        m.coef = sb("coef", [P, 8])
        m.smat = sb("smat", [P, 8, 8])
        m.basew = sb("basew", [P, 1])
        m.scaler = sb("scaler", [P, 1])

        m.onehot = sb("onehot", [KEYS, ONEHOT_W])
        bias_dram = nc.dram_tensor("bias_rows_dram", (BIAS_ROWS, BIAS_ROW), F32, kind="Internal").ap()

        load_and_turn(nc, m, locals())
        bias_rows0(nc, m, bias_dram)
        group_norm_stats(nc, m, "0")
        for b in range(B):
            attention0(nc, m, b, mask_dram, bias_dram)
        group_norm_stats(nc, m, "1")
        blur1(nc, m)
        group_norm_stats(nc, m, "2")
        attention2(nc, m)
        group_norm_stats(nc, m, "3")
        attention3(nc, m)

        stored = ctx.enter_context(nc.semaphore("stored"))
        with nc.Block() as block:
            @block.sync
            def _(sp):
                for u in range(UNITS):
                    sp.dma_start(out[u // 2, (u % 2) * P:(u % 2 + 1) * P].rearrange("c h w -> c (h w)"), m.X[:, u, :]).then_inc(stored, 16)
                sp.wait_ge(stored, 16 * UNITS)


def load_and_turn(nc, m, a):
    with ExitStack() as st:
        sem = st.enter_context(signals(nc, "load"))
        wnat = st.enter_context(nc.sbuf_tensor("wnat", [P, W_BLOCKS, P], F32))
        turned = [st.enter_context(nc.psum_tensor(f"turned{i}", [P, 4, P], F32)) for i in range(2)]
        x_loaded, w_loaded, small_loaded = sem("x_loaded"), sem("w_loaded"), sem("small_loaded")
        tables_made, w_turned, w_copied = sem("tables_made"), sem("w_turned"), sem("w_copied")
        with nc.Block() as block:
            @block.sync
            def _(sp):
                for w, at, blocks in ((a["qkv_w"], W_QKV, 6), (a["proj_w"], W_PROJ, 2), (a["theta_w"], W_THETA, 1),
                                      (a["phi_w"], W_PHI, 1), (a["g_w"], W_G, 1), (a["wq3"], W_Q3, 1),
                                      (a["wk3"], W_K3, 1), (a["wv3"], W_V3, 1)):
                    sp.dma_start(wnat[:, at:at + 2 * blocks, :].rearrange("p (o i) c -> p o (i c)", o=blocks),
                                 w.rearrange("(o p) c -> p o c", p=P)).then_inc(w_loaded, 16)
                for w, at in ((a["out_w"], W_OUT), (a["wo3"], W_O3)):
                    sp.dma_start(wnat[:, at:at + 2, :], w.rearrange("(o p) c -> p o c", p=P)).then_inc(w_loaded, 16)
                for u in range(UNITS):
                    sp.dma_start(m.X[:, u, :], a["x"][u // 2, (u % 2) * P:(u % 2 + 1) * P].rearrange("c h w -> c (h w)")).then_inc(x_loaded, 16)
                sp.wait_ge(x_loaded, 16 * UNITS)

            @block.scalar
            def _(act):
                smalls = [(m.qkvb[:, :], a["qkv_b"].rearrange("(o p) -> p o", p=P)),
                          (m.pbias[:, :], a["proj_b"].rearrange("(o p) -> p o", p=P)),
                          (m.vbias[:, :], a["qkv_b"][2 * HALVES * P:].partition_broadcast(P)),
                          (m.fir[:, :], a["fir"].rearrange("a b -> (a b)").partition_broadcast(P)),
                          (m.cfc[:, :, :], a["cfc"].rearrange("(o p) t -> p o t", p=P)),
                          (m.bias2[:, 0:1], a["theta_b"].rearrange("(p o) -> p o", o=1)),
                          (m.bias2[:, 1:2], a["phi_b"].rearrange("(p o) -> p o", o=1)),
                          (m.bias2[:, 2:4], a["out_b"].rearrange("(o p) -> p o", p=P)),
                          (m.gbias[:, :], a["g_b"].partition_broadcast(P)),
                          (m.coef[:, :], a["spline_w"].rearrange("a b k -> (a b k)").partition_broadcast(P)),
                          (m.smat[:, :, :].rearrange("p a b -> p (a b)"), a["spline_m"].rearrange("a b -> (a b)").partition_broadcast(P)),
                          (m.basew[:, :], a["base_w"].rearrange("a b -> (a b)").partition_broadcast(P)),
                          (m.scaler[:, :], a["spline_scaler"].rearrange("a b -> (a b)").partition_broadcast(P))]
                for kh in range(WS):
                    smalls.append((m.rb[kh * WS:(kh + 1) * WS].rearrange("k a b h -> k a (b h)"),
                                   bass.AP(a["rel_bias"].tensor, kh * (2 * WS - 1) * HEADS0,
                                           [[HEADS0, WS], [(2 * WS - 1) * HEADS0, WS], [1, WS * HEADS0]])))
                for dst, src in smalls:
                    act.dma_start(dst, src, allow_slow_non_contiguous=True).then_inc(small_loaded, 16)
                act.wait_ge(small_loaded, 16 * len(smalls))

            @block.gpsimd
            def _(pool):
                pool.memset(m.ident[:, :], 0.0).then_inc(tables_made, 1)
                pool.memset(m.group[:, :], 1.0 / 8).then_inc(tables_made, 1)
                pool.wait_ge(tables_made, 2)
                pool.affine_select(out=m.ident[:, :], in_=m.ident[:, :], compare_op=ALU.not_equal, fill=1.0, base=0,
                                   pattern=[[-1, P]], channel_multiplier=1).then_inc(tables_made, 1)
                g3 = m.group[:, :].rearrange("p (g c) -> p g c", c=8)
                pool.affine_select(out=g3, in_=g3, compare_op=ALU.is_ge, fill=0.0, base=0,
                                   pattern=[[-8, 16], [0, 8]], channel_multiplier=1).then_inc(tables_made, 1)
                pool.wait_ge(tables_made, 4)
                pool.affine_select(out=g3, in_=g3, compare_op=ALU.is_ge, fill=0.0, base=7,
                                   pattern=[[8, 16], [0, 8]], channel_multiplier=-1).then_inc(tables_made, 1)
                pool.wait_ge(tables_made, 5)

            @block.tensor
            def _(pe):
                pe.wait_ge(tables_made, 5)
                pe.wait_ge(w_loaded, 160)
                for n in range(W_BLOCKS // 4):
                    if n >= 2:
                        pe.wait_ge(w_copied, n - 1)
                    for j in range(4):
                        t = pe.transpose(turned[n % 2][:, j, :], wnat[:, 4 * n + j, :], m.ident[:, :])
                    t.then_inc(w_turned, 1)

            @block.vector
            def _(dve):
                for n in range(W_BLOCKS // 4):
                    dve.wait_ge(w_turned, n + 1)
                    dve.tensor_copy(m.WT[:, 4 * n:4 * n + 4, :], turned[n % 2][:, :, :]).then_inc(w_copied, 1)
                dve.wait_ge(w_copied, W_BLOCKS // 4)


def group_norm_stats(nc, m, tag):
    with ExitStack() as st:
        sem = st.enter_context(signals(nc, tag))
        sb = lambda name, shape: st.enter_context(nc.sbuf_tensor(name + tag, shape, F32))
        stats = sb("stats", [P, UNITS, CHUNKS, 6])
        sq = sb("sq", [P, UNITS])
        e2 = sb("e2", [P, UNITS, 2])
        gst = sb("gst", [P, UNITS, 2])
        gsq = sb("gsq", [P, UNITS])
        gvar = sb("gvar", [P, UNITS])
        geps = sb("geps", [P, UNITS])
        gstd = sb("gstd", [P, UNITS])
        gp = st.enter_context(nc.psum_tensor("gp" + tag, [P, 2 * UNITS], F32))
        chain, moments, grouped, var_ready, std_ready = (sem(n) for n in ("gn_chain", "gn_moments", "gn_grouped", "gn_var", "gn_std"))
        with nc.Block() as block:
            @block.vector
            def _(dve):
                done = [0]

                def link(ins):
                    done[0] += 1
                    ins.then_inc(chain, 1)

                for u in range(UNITS):
                    for k in range(CHUNKS):
                        link(dve.bn_stats(stats[:, u, k, :], m.X[:, u, CHUNK * k:CHUNK * (k + 1)]))
                dve.wait_ge(chain, done[0])
                for u in range(UNITS):
                    link(dve.bn_aggr(m.mv[:, u, :], stats[:, u, :, :].rearrange("p k s -> p (k s)")))
                dve.wait_ge(chain, done[0])
                link(dve.tensor_tensor(sq[:, :], m.mv[:, :, 0], m.mv[:, :, 0], ALU.mult))
                dve.wait_ge(chain, done[0])
                dve.tensor_copy(e2[:, :, 0], m.mv[:, :, 0]).then_inc(moments, 1)
                dve.tensor_tensor(e2[:, :, 1], sq[:, :], m.mv[:, :, 1], ALU.add).then_inc(moments, 1)
                dve.wait_ge(grouped, 1)
                link(dve.tensor_copy(gst[:, :, :].rearrange("p u s -> p (u s)"), gp[:, :]))
                dve.wait_ge(chain, done[0])
                link(dve.tensor_tensor(gsq[:, :], gst[:, :, 0], gst[:, :, 0], ALU.mult))
                dve.wait_ge(chain, done[0])
                link(dve.tensor_tensor(gvar[:, :], gst[:, :, 1], gsq[:, :], ALU.subtract))
                dve.wait_ge(chain, done[0])
                dve.tensor_scalar(geps[:, :], gvar[:, :], GN_EPS, None, ALU.add).then_inc(var_ready, 1)
                dve.wait_ge(std_ready, 1)
                link(dve.reciprocal(m.rstd[:, :], gstd[:, :]))
                dve.wait_ge(chain, done[0])
                link(dve.scalar_tensor_tensor(m.nbias[:, :], gst[:, :, 0], -1.0, m.rstd[:, :], ALU.mult, ALU.mult))
                dve.wait_ge(chain, done[0])

            @block.tensor
            def _(pe):
                pe.wait_ge(moments, 2)
                pe.matmul(gp[:, :], m.group[:, :], e2[:, :, :].rearrange("p u s -> p (u s)"), start=True, stop=True).then_inc(grouped, 1)

            @block.scalar
            def _(act):
                act.wait_ge(var_ready, 1)
                act.activation(gstd[:, :], geps[:, :], ACT.Sqrt).then_inc(std_ready, 1)
                act.wait_ge(std_ready, 1)


def bias_rows0(nc, m, bias_dram):
    with ExitStack() as st:
        sem = st.enter_context(signals(nc, "bias"))
        rows = [st.enter_context(nc.sbuf_tensor(f"bias_rows{k}", [P, BIAS_ROW], F32)) for k in range(2)]
        rp = [st.enter_context(nc.psum_tensor(f"bias_rows_psum{k}", [P, 512], F32)) for k in range(2)]
        table, laid_out, copied, stored = sem("onehot_made"), sem("bias_laid_out"), sem("bias_rows_copied"), sem("bias_rows_stored")
        blocks = ((0, P), (P, BIAS_ROWS - P))
        with nc.Block() as block:
            @block.gpsimd
            def _(pool):
                pool.memset(m.onehot[:, :], 0.0).then_inc(table, 1)
                pool.wait_ge(table, 1)
                pool.affine_select(out=m.onehot[:, :], in_=m.onehot[:, :], compare_op=ALU.not_equal, fill=1.0, base=-ONEHOT_OFF,
                                   pattern=[[1, ONEHOT_W]], channel_multiplier=-1).then_inc(table, 1)

            @block.tensor
            def _(pe):
                pe.wait_ge(table, 2)
                for k, (u0, nu) in enumerate(blocks):
                    def place(s):
                        return m.onehot[:, ONEHOT_OFF + u0 + s:ONEHOT_OFF + u0 + s + nu]
                    for dy in range(WS):
                        for w in range(WIN):
                            at = (dy * WIN + w) * HEADS0
                            pe.matmul(rp[k][0:nu, at:at + HEADS0], place(6 * dy - KEYS * w), m.rb[:, 3, 3, :], start=True, stop=True)
                    for w in range(WIN):
                        for side in range(2):
                            at = (WS * WIN + w * 6 + 3 * side) * HEADS0
                            mm = pe.matmul(rp[k][0:nu, at:at + 3 * HEADS0], place(36 * side - KEYS * w),
                                           m.rb[:, 4 * side:4 * side + 3, 3, :], start=True, stop=True)
                    mm.then_inc(laid_out, 1)

            @block.vector
            def _(dve):
                for k, (u0, nu) in enumerate(blocks):
                    dve.wait_ge(laid_out, k + 1)
                    dve.tensor_copy(rows[k][0:nu, :], rp[k][0:nu, 0:BIAS_ROW]).then_inc(copied, 1)

            @block.sync
            def _(sp):
                for k, (u0, nu) in enumerate(blocks):
                    sp.wait_ge(copied, k + 1)
                    sp.dma_start(bias_dram[u0:u0 + nu, :], rows[k][0:nu, :]).then_inc(stored, 16)
                sp.wait_ge(stored, 32)


def attention0(nc, m, b, mask_dram, bias_dram):
    scale = float(HD0) ** -0.5
    with ExitStack() as outer:
        keep = lambda name, shape: outer.enter_context(nc.sbuf_tensor(f"{name}_{b}", shape, F32))
        xn = keep("xn0", [P, HALVES, L])
        Q = keep("Q0", [P, HALVES, QCOLS])
        O = keep("O0", [P, HALVES, QCOLS])
        qb = keep("qb0", [P, HALVES])

        project_queries0(nc, m, b, xn, Q, O, qb, scale)
        row_pairs0(nc, m, b, xn, Q, O, mask_dram, bias_dram)
        border0(nc, m, b, xn, Q, O)
        project_out0(nc, m, b, O)


def project_queries0(nc, m, b, xn, Q, O, qb, scale):
    with ExitStack() as st:
        sem = st.enter_context(signals(nc, f"p0_{b}"))
        qp = [st.enter_context(nc.psum_tensor(f"qp{i}_{b}", [P, 8, IMG], F32)) for i in range(4)]
        normed, cleared, q_made, q_placed, qb_ready = (sem(n) for n in ("xn_ready", "cleared", "q_made", "q_placed", "qb_ready"))
        with nc.Block() as block:
            @block.vector
            def _(dve):
                for i in range(HALVES):
                    u = HALVES * b + i
                    dve.tensor_scalar(xn[:, i, :], m.X[:, u, :], m.rstd[:, u:u + 1], m.nbias[:, u:u + 1], ALU.mult, ALU.add).then_inc(normed, 1)
                dve.tensor_scalar(qb[:, :], m.qkvb[:, 0:2], scale, None, ALU.mult).then_inc(qb_ready, 1)
                dve.memset(O[:, :, :], 0.0).then_inc(cleared, 1)

            @block.gpsimd
            def _(pool):
                pool.memset(Q[:, :, GRID * GRID:PAIR0 + 6], 0.0).then_inc(cleared, 1)
                pool.memset(Q[:, :, CORNER0 - 6:CORNER0], 0.0).then_inc(cleared, 1)

            @block.tensor
            def _(pe):
                pe.wait_ge(normed, HALVES)
                for n in range(HALVES * CHUNKS):
                    k, o = n // HALVES, n % HALVES
                    if n >= 4:
                        pe.wait_ge(q_placed, n - 3)
                    for i in range(HALVES):
                        mm = pe.matmul(qp[n % 4][:, :, :].rearrange("p r c -> p (r c)"), m.WT[:, W_QKV + 2 * o + i, :],
                                       xn[:, i, CHUNK * k:CHUNK * (k + 1)], start=(i == 0), stop=(i == HALVES - 1))
                    mm.then_inc(q_made, 1)

            @block.scalar
            def _(act):
                act.wait_ge(qb_ready, 1)
                act.wait_ge(cleared, 3)
                for n in range(HALVES * CHUNKS):
                    k, o = n // HALVES, n % HALVES
                    act.wait_ge(q_made, n + 1)
                    placed = [None]

                    def place(dst, rows, cols):
                        src = qp[n % 4][:, rows[0] - 8 * k:rows[1] - 8 * k, cols[0]:cols[1]]
                        placed[0] = act.activation(dst, src, ACT.Identity, bias=qb[:, o:o + 1], scale=scale)

                    def span(at, rows, row_step, cols):
                        return Q[:, o, at:at + rows * row_step].rearrange("p (r c) -> p r c", c=row_step)[:, :, 0:cols]

                    r0, r1 = max(3, 8 * k), min(53, 8 * k + 8)
                    place(span((r0 - 3) * GRID, r1 - r0, GRID, GRID), (r0, r1), (3, 53))
                    place(span(PAIR0 + 6 * (r0 - 3) + 3, r1 - r0, 6, 3), (r0, r1), (0, 3))
                    place(span(PAIR0 + 6 * (r0 - 2), r1 - r0, 6, 3), (r0, r1), (53, 56))
                    if k == 0:
                        place(span(EXTRA + DX_STEP, 3, DX_STEP, GRID), (0, 3), (3, 53))
                        place(span(CORNER0, 4, 3, 3), (0, 4), (0, 3))
                        place(span(CORNER0 + 12, 4, 3, 3), (0, 4), (53, 56))
                    if k == CHUNKS - 1:
                        place(span(EXTRA + 4 * DX_STEP + BOTTOM_SHIFT, 3, DX_STEP, GRID), (53, 56), (3, 53))
                        place(span(CORNER0 + 24, 4, 3, 3), (52, 56), (0, 3))
                        place(span(CORNER0 + 36, 4, 3, 3), (52, 56), (53, 56))
                    placed[0].then_inc(q_placed, 1)
                act.wait_ge(q_placed, HALVES * CHUNKS)


def row_pairs0(nc, m, b, xn, Q, O, mask_dram, bias_dram):
    with ExitStack() as st:
        sem = st.enter_context(signals(nc, f"a0_{b}"))
        sb = lambda name, shape: st.enter_context(nc.sbuf_tensor(f"{name}_{b}", shape, F32))
        ps = lambda name, shape: st.enter_context(nc.psum_tensor(f"{name}_{b}", shape, F32))
        xt = [sb(f"xt{r}", [P, HALVES, TILE]) for r in range(2)]
        qt = [sb(f"qt{r}", [P, HALVES, COLS]) for r in range(2)]
        kt = [sb(f"kt{r}", [P, HALVES, TILE]) for r in range(2)]
        vt = [sb(f"vt{r}", [TILE, HALVES * P]) for r in range(2)]
        rows = [sb(f"rows{r}", [TILE, BIAS_ROW]) for r in range(2)]
        mask = [sb(f"mask{r}", [TILE, COLS]) for r in range(2)]
        bias = [sb(f"bias{r}", [TILE, 4, HALVES, COLS]) for r in range(2)]
        A = [sb(f"A{r}", [TILE, 4, HALVES, COLS]) for r in range(2)]
        kvp = [ps(f"kvp{r}", [P, 512]) for r in range(2)]
        scp = ps("scp", [P, 4, 512])
        op = ps("op", [P, 512])
        xt_ready, qt_ready, kv_ready, bias_ready, scores_made, o_made, o_added, bias_zeroed = (
            sem(n) for n in ("xt_ready", "qt_ready", "kv_ready", "bias_ready", "scores_made", "o_made", "o_added", "bias_zeroed"))
        tables_loaded = [sem(f"tables_loaded{r}") for r in range(2)]
        kv_made, scores_added, masked = (sem(n) for n in ("kv_made", "scores_added", "masked"))

        def ramp(eng, front, back):
            front(eng, 0, 0, 0)
            with eng.Fori(0, (TILES - 2) // 2) as i:
                for k in (1, 2):
                    front(eng, 2 * i + k, k % 2, i + k // 2)
                    back(eng, 2 * i + (k - 1), (k - 1) % 2, i)
            front(eng, TILES - 1, 1, TILES // 2 - 1)
            back(eng, TILES - 2, 0, TILES // 2 - 1)
            back(eng, TILES - 1, 1, TILES // 2 - 1)

        def nothing(eng, t, r, turn):
            pass

        def block_cols(view, t):
            return bass.AP(view.tensor, view.offset + 2 * t, [view.ap[0], [DY_STEP, WS + 1], [DX_STEP, WS], [1, WIN]])

        def fixed_cols(view):
            return view.rearrange("p (y x w) -> p y x w", y=WS + 1, x=WS)

        with nc.Block() as block:
            @block.sync
            def _(sp):
                def load(eng, t, r, turn):
                    eng.wait_ge(masked, t + 1)
                    eng.dma_start(mask[r][:, :], mask_dram[bass.ds(t, 1)].rearrange("t p c -> p (t c)")).then_inc(tables_loaded[r], 16)
                    eng.wait_ge(bias_ready, t + 1)
                    for q in range(2):
                        eng.dma_start(rows[r][q * IMG:(q + 1) * IMG, :], bias_dram[bass.ds(2 * t + GRID * q, IMG), :]).then_inc(tables_loaded[r], 16)
                ramp(sp, load, nothing)

            @block.scalar
            def _(act):
                def stage(eng, t, r, turn):
                    eng.wait_ge(kv_made, t + 1)
                    eng.activation(xt[r][:, :, :], xn[:, :, bass.ds(TILE * t, TILE)], ACT.Copy).then_inc(xt_ready, 1)
                    eng.wait_ge(tables_loaded[r], 48 * (turn + 1))
                    eng.wait_ge(scores_added, t + 1)
                    for h in range(4):
                        for f in range(HALVES):
                            dst = bias[r][:, h, f, 0:WS * WS * WIN].rearrange("p (y x w) -> p y x w", y=WS, x=WS)
                            src = rows[r][:, 0:WS * WIN * HEADS0].rearrange("p (y w e) -> p y w e", y=WS, w=WIN)[:, :, :, 4 * f + h]
                            eng.activation(dst, src.unsqueeze(2).to_broadcast([TILE, WS, WS, WIN]), ACT.Copy)
                    for f in range(HALVES):
                        for w in range(WIN):
                            dst = bias[r][:, :, f, WS * WS * WIN:].rearrange("p h (x w) -> p h x w", w=WIN)[:, :, 1:WS, w]
                            at = WS * WIN * HEADS0 + w * 6 * HEADS0
                            src = rows[r][:, at:at + 6 * HEADS0].rearrange("p (s e) -> p e s", e=HEADS0)[:, 4 * f:4 * f + 4, :]
                            last = eng.activation(dst, src, ACT.Copy)
                    last.then_inc(bias_ready, 1)
                act.wait_ge(bias_zeroed, 2)
                ramp(act, stage, nothing)

            @block.gpsimd
            def _(pool):
                def stage(eng, t, r, turn):
                    eng.wait_ge(scores_added, t + 1)
                    for f in range(HALVES):
                        eng.tensor_copy(fixed_cols(qt[r][:, f, :]), block_cols(Q[:, f, :], t)).then_inc(qt_ready, 1)

                def apply_mask(eng, t, r, turn):
                    eng.wait_ge(tables_loaded[r], 48 * (turn + 1))
                    eng.wait_ge(scores_added, t + 3)
                    a = A[r][:, :, :, :].rearrange("p h f c -> p (h f) c")
                    eng.tensor_tensor(a, a, mask[r][:, :].unsqueeze(1).to_broadcast([TILE, 8, COLS]), ALU.mult).then_inc(masked, 1)

                pool.sem_inc(masked, 2)
                for r in range(2):
                    pool.memset(bias[r][:, :, :, WS * WS * WIN:].rearrange("p h f c -> p (h f) c"), 0.0).then_inc(bias_zeroed, 1)
                ramp(pool, stage, apply_mask)

            @block.tensor
            def _(pe):
                def front(eng, t, r, turn):
                    eng.wait_ge(xt_ready, t + 1)
                    eng.wait_ge(kv_ready, 3 * (t + 1))
                    for f in range(HALVES):
                        for i in range(HALVES):
                            eng.matmul(kvp[r][:, f * TILE:(f + 1) * TILE], m.WT[:, W_QKV + 2 * (2 + f) + i, :], xt[r][:, i, :],
                                       start=(i == 0), stop=(i == HALVES - 1))
                    for i in range(HALVES):
                        mm = eng.matmul(kvp[r][0:TILE, 2 * TILE:2 * TILE + 2 * P], xt[r][:, i, :],
                                        m.WT[:, W_QKV + 8 + i:W_QKV + 12:2, :], start=(i == 0), stop=(i == HALVES - 1))
                    mm.then_inc(kv_made, 1)
                    eng.wait_ge(kv_ready, 3 * (t + 3))
                    eng.wait_ge(qt_ready, HALVES * (t + 1))
                    eng.wait_ge(scores_added, t + 2)
                    for f in range(HALVES):
                        for h in range(4):
                            rows = slice(HD0 * h, HD0 * (h + 1))
                            mm = eng.matmul(scp[0:TILE, h, f * COLS:(f + 1) * COLS], kt[r][rows, f, :], qt[r][rows, f, :], start=True, stop=True)
                    mm.then_inc(scores_made, 1)

                def back(eng, t, r, turn):
                    eng.wait_ge(masked, t + 3)
                    eng.wait_ge(o_added, HALVES * (t + 1))
                    for f in range(HALVES):
                        for h in range(4):
                            rows = slice(HD0 * h, HD0 * (h + 1))
                            mm = eng.matmul(op[rows, f * COLS:(f + 1) * COLS], vt[r][:, f * P + HD0 * h:f * P + HD0 * (h + 1)],
                                            A[r][:, h, f, :], start=True, stop=True)
                    mm.then_inc(o_made, 1)

                pe.sem_inc(kv_made, 2)
                ramp(pe, front, back)

            @block.vector
            def _(dve):
                def front(eng, t, r, turn):
                    eng.wait_ge(kv_made, t + 3)
                    for f in range(HALVES):
                        eng.tensor_scalar(kt[r][:, f, :], kvp[r][:, f * TILE:(f + 1) * TILE], m.qkvb[:, 2 + f:3 + f], None, ALU.add).then_inc(kv_ready, 1)
                    eng.tensor_tensor(vt[r][:, :], kvp[r][0:TILE, 2 * TILE:2 * TILE + 2 * P], m.vbias[0:TILE, :], ALU.add).then_inc(kv_ready, 1)
                    eng.wait_ge(scores_made, t + 1)
                    eng.wait_ge(bias_ready, t + 3)
                    eng.tensor_tensor(A[r][:, :, :, :].rearrange("p h f c -> p h (f c)"), scp[0:TILE, :, 0:HALVES * COLS],
                                      bias[r][:, :, :, :].rearrange("p h f c -> p h (f c)"), ALU.add).then_inc(scores_added, 1)

                def back(eng, t, r, turn):
                    eng.wait_ge(o_made, t + 1)
                    eng.wait_ge(o_added, HALVES * (t + 1))
                    for f in range(HALVES):
                        dst = block_cols(O[:, f, :], t)
                        eng.tensor_tensor(dst, dst, fixed_cols(op[:, f * COLS:(f + 1) * COLS]), ALU.add).then_inc(o_added, 1)

                dve.sem_inc(kv_ready, 6)
                dve.sem_inc(scores_added, 2)
                dve.sem_inc(o_added, HALVES)
                dve.sem_inc(bias_ready, 2)
                ramp(dve, front, back)
                dve.wait_ge(o_added, HALVES * (TILES + 1))


def border0(nc, m, b, xn, Q, O):
    with ExitStack() as st:
        sem = st.enter_context(signals(nc, f"a0_{b}"))
        sb = lambda name, shape: st.enter_context(nc.sbuf_tensor(f"{name}_{b}", shape, F32))
        ps = lambda name, shape: st.enter_context(nc.psum_tensor(f"{name}_{b}", shape, F32))
        n7 = WS * PAIR_W
        xe = sb("xe", [P, HALVES, n7])
        ke = sb("ke", [P, HALVES, n7])
        ve = sb("ve", [PAIR_W, 8, HALVES * P])
        qe = sb("qe", [P, HALVES, WS, 4, 6])
        qc = sb("qc", [P, HALVES, 4, 4, 12])
        ae = sb("ae", [PAIR_W, WS, HALVES, 4, 6])
        emask = sb("emask", [PAIR_W, HALVES, 2, 3])
        ebias = sb("ebias", [PAIR_W, HALVES, 4, 6])
        cbias = sb("cbias", [KEYS, 4, HALVES, 4, 12])
        ca = sb("ca", [KEYS, 4, HALVES, 4, 12])
        kp = ps("kpe", [P, 4, 512])
        vp = ps("vpe", [P, 4, 512])
        q_zeroed, eb_made, eb_ready, mask_made, xe_ready, qe_ready, kv_made, kv_ready, s_made, s_masked, a_ready, o_made, o_placed = (
            sem("e_" + n) for n in ("q_zeroed", "eb_made", "eb_ready", "mask_made", "xe_ready", "qe_ready", "kv_made", "kv_ready", "s_made", "s_masked", "a_ready", "o_made", "o_placed"))
        GROUPS = WS + 1

        def k_parts(total):
            return [(0, total)] if total <= 512 else [(0, total // 2), (total // 2, total)]

        with nc.Block() as block:
            @block.gpsimd
            def _(pool):
                for rows in (qe, qc):
                    pool.memset(rows[:, :, :, :, :].rearrange("p f w h q -> p (f w h q)"), 0.0).then_inc(q_zeroed, 1)
                pool.memset(emask[:, :, :, :].rearrange("p f s q -> p (f s q)"), 1.0).then_inc(mask_made, 1)
                pool.wait_ge(mask_made, 1)
                left, right = emask[:, :, 1, :], emask[:, :, 0, :]
                pool.affine_select(out=right, in_=right, compare_op=ALU.is_ge, fill=0.0, base=KEYS - 1, pattern=[[0, HALVES], [0, 3]],
                                   channel_multiplier=-1).then_inc(mask_made, 1)
                pool.affine_select(out=left, in_=left, compare_op=ALU.is_ge, fill=0.0, base=-(IMG - 1), pattern=[[0, HALVES], [0, 3]],
                                   channel_multiplier=1).then_inc(mask_made, 1)

            @block.scalar
            def _(act):
                def group(eng, g, n, width, nq, xsrc, qat):
                    eng.activation(xe[:, :, 0:n * width].rearrange("p f (n w) -> p f n w", n=n), xsrc, ACT.Copy).then_inc(xe_ready, 1)
                    for h in range(4):
                        rows = slice(HD0 * h, HD0 * (h + 1))
                        eng.activation(qe[rows, :, :, h, :], Q[rows, :, bass.ds(qat, n * nq)].rearrange("p f (n q) -> p f n q", n=n), ACT.Copy).then_inc(qe_ready, 1)
                    eng.wait_ge(o_made, g + 1)
                    src = vp[:, 0, 0:HALVES * n * nq].rearrange("p (f q) -> p f q", f=HALVES)
                    eng.activation(O[:, :, bass.ds(qat, n * nq)], src, ACT.Copy).then_inc(o_placed, 1)

                view = xn[:, :, :]
                act.wait_ge(q_zeroed, 2)
                with act.Fori(0, WS) as dy:
                    src = bass.AP(view.tensor, view.offset + (48 * IMG + 1 - 55 * (WS - 1)) - 336 * dy, [view.ap[0], [L, HALVES], [IMG - 1, WS], [1, PAIR_W]])
                    group(act, dy, WS, PAIR_W, 6, src, PAIR0 + 6 + 42 * dy)
                for c in range(4):
                    act.activation(xe[:, :, c * KEYS:(c + 1) * KEYS], xn[:, :, CORNER_PIX[c]:CORNER_PIX[c] + KEYS], ACT.Copy).then_inc(xe_ready, 1)
                for h in range(4):
                    rows = slice(HD0 * h, HD0 * (h + 1))
                    act.activation(qc[rows, :, :, h, :], Q[rows, :, CORNER0:CORNER0 + 48].rearrange("p f (n q) -> p f n q", n=4), ACT.Copy).then_inc(qe_ready, 1)
                act.wait_ge(o_made, GROUPS)
                act.activation(O[:, :, CORNER0:CORNER0 + 48], vp[:, 0, 0:96].rearrange("p (f q) -> p f q", f=HALVES), ACT.Copy).then_inc(o_placed, 1)
                act.wait_ge(o_placed, GROUPS)

            @block.tensor
            def _(pe):
                for side in range(2):
                    at = ONEHOT_OFF - (IMG - 1) * side
                    c0 = 4 - 4 * side
                    mm = pe.matmul(kp[0:PAIR_W, 0, 24 * side:24 * side + 24], m.onehot[:, at:at + PAIR_W], m.rb[:, 3, c0:c0 + 3, :], start=True, stop=True)
                for c in range(4):
                    r0, c0 = 3 * (c // 2), 4 * (c % 2)
                    mm = pe.matmul(vp[0:KEYS, 0, 96 * c:96 * c + 96], m.onehot[:, ONEHOT_OFF:ONEHOT_OFF + KEYS],
                                   m.rb[:, r0:r0 + 4, c0:c0 + 3, :].rearrange("k a b h -> k a (b h)"), start=True, stop=True)
                mm.then_inc(eb_made, 1)
                pe.wait_ge(eb_ready, 5)

                def group(eng, g, n, width, nq, xe_count):
                    eng.wait_ge(xe_ready, xe_count)
                    parts = k_parts(n * width)
                    slot = lambda w: n - 1 - w if nq == 6 else w
                    for f in range(HALVES):
                        for j, (a, z) in enumerate(parts):
                            for i in range(HALVES):
                                eng.matmul(kp[:, 2 * f + j, 0:z - a], m.WT[:, W_QKV + 2 * (2 + f) + i, :], xe[:, i, a:z],
                                           start=(i == 0), stop=(i == HALVES - 1))
                    for w in range(n):
                        for i in range(HALVES):
                            mm = eng.matmul(vp[0:width, w // 2, 2 * P * (w % 2):2 * P * (w % 2 + 1)], xe[:, i, w * width:(w + 1) * width],
                                            m.WT[:, W_QKV + 8 + i:W_QKV + 12:2, :], start=(i == 0), stop=(i == HALVES - 1))
                    mm.then_inc(kv_made, 1)
                    eng.wait_ge(qe_ready, 4 * (g + 1))
                    eng.wait_ge(kv_ready, g + 1)
                    for w in range(n):
                        for f in range(HALVES):
                            at = (w * HALVES + f) * 4 * nq
                            mm = eng.matmul(kp[0:width, 0, at:at + 4 * nq], ke[:, f, slot(w) * width:(slot(w) + 1) * width],
                                            (qe if nq == 6 else qc)[:, f, w, :, :].rearrange("p h q -> p (h q)"), start=True, stop=True)
                    mm.then_inc(s_made, 1)
                    eng.wait_ge(a_ready, g + 1)
                    for w in range(n):
                        for f in range(HALVES):
                            for h in range(4):
                                rows = slice(HD0 * h, HD0 * (h + 1))
                                rhs = (ae if nq == 6 else ca)[:, w, f, h, :]
                                at = f * n * nq + w * nq
                                mm = eng.matmul(vp[rows, 0, at:at + nq], ve[0:width, slot(w), f * P + HD0 * h:f * P + HD0 * (h + 1)], rhs, start=True, stop=True)
                    mm.then_inc(o_made, 1)
                    eng.wait_ge(o_placed, g + 1)

                with pe.Fori(0, WS) as dy:
                    group(pe, dy, WS, PAIR_W, 6, dy + 1)
                group(pe, WS, 4, KEYS, 12, WS + 4)

            @block.vector
            def _(dve):
                dve.wait_ge(eb_made, 1)
                dve.tensor_copy(ebias[:, :, :, :], kp[0:PAIR_W, 0, 0:48].rearrange("p (q f h) -> p f h q", q=6, f=HALVES)).then_inc(eb_ready, 1)
                for c in range(4):
                    src = vp[0:KEYS, 0, 96 * c:96 * c + 96].rearrange("p (q f h) -> p f h q", q=12, f=HALVES)
                    dve.tensor_copy(cbias[:, c, :, :, :], src).then_inc(eb_ready, 1)
                dve.wait_ge(eb_ready, 5)
                dve.wait_ge(mask_made, 3)

                def kv(eng, g, n, width):
                    eng.wait_ge(kv_made, g + 1)
                    for f in range(HALVES):
                        for j, (a, z) in enumerate(k_parts(n * width)):
                            eng.tensor_scalar(ke[:, f, a:z], kp[:, 2 * f + j, 0:z - a], m.qkvb[:, 2 + f:3 + f], None, ALU.add)
                    eng.tensor_tensor(ve[0:width, 0:n, :], vp[0:width, :, :].rearrange("p a (b c) -> p (a b) c", b=2)[:, 0:n, :],
                                      m.vbias[0:width, :].unsqueeze(1).to_broadcast([width, n, HALVES * P]), ALU.add).then_inc(kv_ready, 1)

                with dve.Fori(0, WS) as dy:
                    kv(dve, dy, WS, PAIR_W)
                    dve.wait_ge(s_made, dy + 1)
                    dve.tensor_tensor(ae[:, :, :, :, :].rearrange("p w f h q -> p (w f h) q"),
                                      kp[0:PAIR_W, 0, 0:WS * HALVES * 24].rearrange("p (w q) -> p w q", q=6),
                                      emask[:, 0, :, :].rearrange("p s q -> p (s q)").unsqueeze(1).to_broadcast([PAIR_W, WS * HALVES * 4, 6]),
                                      ALU.mult).then_inc(s_masked, 1)
                    dve.wait_ge(s_masked, dy + 1)
                    by_window = ae[:, :, :, :, :].rearrange("p w f h q -> p w (f h q)")
                    dve.tensor_tensor(by_window, by_window,
                                      ebias[:, :, :, :].rearrange("p f h q -> p (f h q)").unsqueeze(1).to_broadcast([PAIR_W, WS, HALVES * 24]),
                                      ALU.add).then_inc(a_ready, 1)
                kv(dve, WS, 4, KEYS)
                dve.wait_ge(s_made, GROUPS)
                flat = lambda buf: buf[:, :, :, :, :].rearrange("p c f h q -> p (c f h q)")
                dve.tensor_tensor(flat(ca), kp[0:KEYS, 0, 0:384], flat(cbias), ALU.add).then_inc(a_ready, 1)


def project_out0(nc, m, b, O):
    with ExitStack() as st:
        sem = st.enter_context(signals(nc, f"p0_{b}"))
        yp = [st.enter_context(nc.psum_tensor(f"yp{i}_{b}", [P, 512], F32)) for i in range(8)]
        y_made, y_added = sem("y_made"), sem("y_added")
        slots = EXTRA + DX_STEP
        spans = [(500 * k, 500) for k in range(5)] + [(slots, 314), (PAIR0 + 6, 294), (CORNER0, 48)]
        with nc.Block() as block:
            @block.tensor
            def _(pe):
                for n in range(2 * len(spans)):
                    f, (at, w) = n % 2, spans[n // 2]
                    if n >= 8:
                        pe.wait_ge(y_added, n - 7)
                    for i in range(HALVES):
                        mm = pe.matmul(yp[n % 8][:, 0:w], m.WT[:, W_PROJ + 2 * f + i, :], O[:, i, at:at + w], start=(i == 0), stop=(i == 1))
                    mm.then_inc(y_made, 1)

            @block.vector
            def _(dve):
                for n in range(2 * len(spans)):
                    f, k = n % 2, n // 2
                    dve.wait_ge(y_made, n + 1)
                    X = m.X[:, HALVES * b + f, :]
                    img = X.rearrange("p (r c) -> p r c", c=IMG)
                    last = [None]

                    def add(dst, src):
                        last[0] = dve.scalar_tensor_tensor(dst, src, m.pbias[:, f:f + 1], dst, ALU.add, ALU.add)

                    def grid(at, rows, step, cols):
                        return yp[n % 8][:, at:at + rows * step].rearrange("p (r c) -> p r c", c=step)[:, :, 0:cols]

                    if k < 5:
                        add(img[:, 3 + 10 * k:13 + 10 * k, 3:53], grid(0, 10, GRID, GRID))
                    elif k == 5:
                        add(img[:, 0:3, 3:53], grid(0, 3, DX_STEP, GRID))
                        add(img[:, 53:56, 3:53], grid(3 * DX_STEP + BOTTOM_SHIFT, 3, DX_STEP, GRID))
                    elif k == 6:
                        add(X[:, 3 * IMG + 53:3 * IMG + 53 + 49 * IMG].rearrange("p (r c) -> p r c", c=IMG)[:, :, 0:6], grid(0, 49, 6, 6))
                    else:
                        add(img[:, 0:4, 0:3], grid(0, 4, 3, 3))
                        add(img[:, 0:3, 53:56], grid(12, 3, 3, 3))
                        add(img[:, 53:56, 0:3], grid(27, 3, 3, 3))
                        add(img[:, 52:56, 53:56], grid(36, 4, 3, 3))
                    last[0].then_inc(y_added, 1)
                dve.wait_ge(y_added, 2 * len(spans))


def blur1(nc, m):
    PAD, KW = 2, 4
    TAPS_PE = 7
    places = [(a, b) for a in range(KW) for b in range(KW)]
    tap = lambda a, b: (KW - 1 - a) * KW + KW - 1 - b
    W = IMG + PAD + 1
    with ExitStack() as st:
        sem = st.enter_context(signals(nc, "blur"))
        pad = [st.enter_context(nc.sbuf_tensor(f"pad{r}", [P, W, W], F32)) for r in range(2)]
        diag = [st.enter_context(nc.sbuf_tensor(f"diag_tap{j}", [P, P], F32)) for j in range(TAPS_PE)]
        sums = [st.enter_context(nc.psum_tensor(f"tap_sums{k}", [P, 512], F32)) for k in range(CHUNKS)]
        cleared, padded, tapped, diag_ready, pe_summed, added = (
            sem(n) for n in ("pad_cleared", "padded", "tapped", "diag_ready", "pe_summed", "unit_added"))
        with nc.Block() as block:
            @block.gpsimd
            def _(pool):
                for r in range(2):
                    pool.memset(pad[r][:, :, :], 0.0).then_inc(cleared, 1)

            @block.scalar
            def _(act):
                for u in range(UNITS):
                    act.wait_ge(cleared, u % 2 + 1)
                    if u >= 2:
                        act.wait_ge(added, CHUNKS * (u - 1))
                    act.activation(pad[u % 2][:, PAD:PAD + IMG, PAD:PAD + IMG], m.X[:, u, :].rearrange("p (r c) -> p r c", c=IMG),
                                   ACT.Identity, bias=m.nbias[:, u:u + 1], scale=m.rstd[:, u:u + 1]).then_inc(padded, 1)

            @block.tensor
            def _(pe):
                pe.wait_ge(diag_ready, TAPS_PE)
                for u in range(UNITS):
                    pe.wait_ge(padded, u + 1)
                    for k in range(CHUNKS):
                        if u:
                            pe.wait_ge(added, CHUNKS * (u - 1) + k + 1)
                        for j, (a, b) in enumerate(places[:TAPS_PE]):
                            mm = pe.matmul(sums[k][:, 0:CHUNK], diag[j][:, :], pad[u % 2][:, a + 8 * k:a + 8 * (k + 1), b:b + IMG],
                                           start=(j == 0), stop=(j == TAPS_PE - 1))
                        mm.then_inc(pe_summed, 1)

            @block.vector
            def _(dve):
                for j, (a, b) in enumerate(places[:TAPS_PE]):
                    t = tap(a, b)
                    dve.tensor_scalar(diag[j][:, :], m.ident[:, :], m.fir[:, t:t + 1], None, ALU.mult).then_inc(diag_ready, 1)
                done = 0
                for u in range(UNITS):
                    img = m.X[:, u, :].rearrange("p (r c) -> p r c", c=IMG)
                    dve.wait_ge(padded, u + 1)
                    for a, b in places[TAPS_PE:]:
                        if done:
                            dve.wait_ge(tapped, done)
                        dve.scalar_tensor_tensor(img, pad[u % 2][:, a:a + IMG, b:b + IMG], m.fir[:, tap(a, b):tap(a, b) + 1], img,
                                                 ALU.mult, ALU.add).then_inc(tapped, 1)
                        done += 1
                    dve.wait_ge(tapped, done)
                    for k in range(CHUNKS):
                        dve.wait_ge(pe_summed, CHUNKS * u + k + 1)
                        X = m.X[:, u, CHUNK * k:CHUNK * (k + 1)]
                        dve.tensor_tensor(X, X, sums[k][:, 0:CHUNK], ALU.add).then_inc(added, 1)
                dve.wait_ge(added, CHUNKS * UNITS)


def pipeline(eng, tiles, stages):
    def step(t, k, known):
        for fn, lag in stages:
            if not known or 0 <= k - lag < tiles:
                fn(eng, t - lag, (k - lag) % 2)
    lags = max(lag for _, lag in stages)
    head = lags + lags % 2
    for k in range(head):
        step(k, k, True)
    turns = (tiles - head) // 2
    with eng.Fori(0, turns) as i:
        for k in (head, head + 1):
            step(2 * i + k, k, False)
    for k in range(head + 2 * turns, tiles + lags):
        step(k, k, True)


def attention2(nc, m):
    with ExitStack() as outer:
        keep = lambda name, shape: outer.enter_context(nc.sbuf_tensor(name, shape, F32))
        gate_scale = keep("gate_scale", [P, UNITS])
        gate_bias = keep("gate_bias", [P, UNITS])
        channel_gate2(nc, m, gate_scale, gate_bias)
        for b in range(B):
            with ExitStack() as st:
                buf = lambda name, shape: st.enter_context(nc.sbuf_tensor(f"{name}_{b}", shape, F32))
                s = buf("gated", [P, HALVES, L])
                theta, phi, nl = buf("theta", [P, L]), buf("phi", [P, L]), buf("nl", [P, L])
                gT = buf("gT", [TILE, TILES, P])
                project2(nc, m, b, s, theta, phi, gT, gate_scale, gate_bias)
                softmax2(nc, m, b, theta, phi, gT, nl)
                project_out2(nc, m, b, s, nl)


def channel_gate2(nc, m, gate_scale, gate_bias):
    with ExitStack() as st:
        sb = lambda name: st.enter_context(nc.sbuf_tensor(name, [P, UNITS], F32))
        mean, scaled, std, z, ez, r2, z0 = (sb("cg_" + n) for n in ("mean", "scaled", "std", "z", "ez", "r2", "z0"))
        sem = st.enter_context(signals(nc, "gate"))
        chain, var_ready, std_ready, z_ready, exp_ready = (sem(n) for n in ("chain", "var_ready", "std_ready", "z_ready", "exp_ready"))

        def both(i):
            return m.cfc[:, :, i].unsqueeze(1).to_broadcast([P, B, HALVES])

        def units(t):
            return t[:, :].rearrange("p (b f) -> p b f", b=B)

        with nc.Block() as block:
            @block.vector
            def _(dve):
                done = [0]

                def link(ins):
                    done[0] += 1
                    ins.then_inc(chain, 1)
                    dve.wait_ge(chain, done[0])
                link(dve.tensor_tensor(mean[:, :], m.mv[:, :, 0], m.rstd[:, :], ALU.mult))
                link(dve.tensor_tensor(mean[:, :], mean[:, :], m.nbias[:, :], ALU.add))
                link(dve.tensor_tensor(r2[:, :], m.rstd[:, :], m.rstd[:, :], ALU.mult))
                link(dve.tensor_tensor(scaled[:, :], m.mv[:, :, 1], r2[:, :], ALU.mult))
                dve.tensor_scalar(scaled[:, :], scaled[:, :], float(L) / (L - 1), 1e-5, ALU.mult, ALU.add).then_inc(var_ready, 1)
                link(dve.tensor_tensor(units(z0), units(mean), both(0), ALU.mult))
                dve.wait_ge(std_ready, 1)
                link(dve.tensor_tensor(units(z), units(std), both(1), ALU.mult))
                dve.tensor_tensor(z[:, :], z[:, :], z0[:, :], ALU.add).then_inc(z_ready, 1)
                dve.wait_ge(exp_ready, 1)
                link(dve.tensor_scalar(ez[:, :], ez[:, :], 1.0, None, ALU.add))
                link(dve.reciprocal(z0[:, :], ez[:, :]))
                link(dve.tensor_tensor(gate_scale[:, :], m.rstd[:, :], z0[:, :], ALU.mult))
                link(dve.tensor_tensor(gate_bias[:, :], m.nbias[:, :], z0[:, :], ALU.mult))

            @block.scalar
            def _(act):
                act.wait_ge(var_ready, 1)
                act.activation(std[:, :], scaled[:, :], ACT.Sqrt).then_inc(std_ready, 1)
                act.wait_ge(z_ready, 1)
                act.activation(ez[:, :], z[:, :], ACT.Exp, scale=-1.0).then_inc(exp_ready, 1)


def project2(nc, m, b, s, theta, phi, gT, gate_scale, gate_bias):
    with ExitStack() as st:
        pp = [st.enter_context(nc.psum_tensor(f"pp{i}_{b}", [P, 512], F32)) for i in range(8)]
        sem = st.enter_context(signals(nc, f"p2_{b}"))
        gated, made, kept_a, kept_v = (sem(n) for n in ("gated", "made", "kept_a", "kept_v"))
        JOBS = 3 * CHUNKS
        with nc.Block() as block:
            @block.vector
            def _(dve):
                for f in range(HALVES):
                    u = HALVES * b + f
                    dve.tensor_scalar(s[:, f, :], m.X[:, u, :], gate_scale[:, u:u + 1], gate_bias[:, u:u + 1], ALU.mult, ALU.add).then_inc(gated, 1)
                for k in range(CHUNKS):
                    dve.wait_ge(made, 3 * k + 3)
                    dve.tensor_tensor(gT[:, 4 * k:4 * k + 4, :], pp[(3 * k + 2) % 8][0:TILE, :].rearrange("p (j c) -> p j c", j=4),
                                      m.gbias[0:TILE, :].unsqueeze(1).to_broadcast([TILE, 4, P]), ALU.add).then_inc(kept_v, 1)
                dve.wait_ge(kept_v, CHUNKS)

            @block.scalar
            def _(act):
                for k in range(CHUNKS):
                    for j, dst in enumerate((theta, phi)):
                        act.wait_ge(made, 3 * k + j + 1)
                        act.activation(dst[:, CHUNK * k:CHUNK * (k + 1)], pp[(3 * k + j) % 8][:, 0:CHUNK], ACT.Identity, bias=m.bias2[:, j:j + 1]).then_inc(kept_a, 1)
                act.wait_ge(kept_a, 2 * CHUNKS)

            @block.tensor
            def _(pe):
                pe.wait_ge(gated, HALVES)
                for n in range(JOBS):
                    k, j = n // 3, n % 3
                    if n >= 8:
                        kk, jj = (n - 8) // 3, (n - 8) % 3
                        if jj == 2:
                            pe.wait_ge(kept_v, kk + 1)
                        else:
                            pe.wait_ge(kept_a, 2 * kk + jj + 1)
                    bank = pp[n % 8]
                    if j < 2:
                        for i in range(HALVES):
                            mm = pe.matmul(bank[:, 0:CHUNK], m.WT[:, (W_THETA, W_PHI)[j] + i, :], s[:, i, CHUNK * k:CHUNK * (k + 1)],
                                           start=(i == 0), stop=(i == 1))
                    else:
                        for q in range(4):
                            at = TILE * (4 * k + q)
                            for i in range(HALVES):
                                mm = pe.matmul(bank[0:TILE, P * q:P * (q + 1)], s[:, i, at:at + TILE], m.WT[:, W_G + i, :],
                                               start=(i == 0), stop=(i == 1))
                    mm.then_inc(made, 1)


def softmax2(nc, m, b, theta, phi, gT, nl):
    SUB2 = L // 8
    with ExitStack() as st:
        sem = st.enter_context(signals(nc, f"a2_{b}"))
        sb = lambda name, shape: st.enter_context(nc.sbuf_tensor(f"a2_{name}_{b}", shape, F32))
        ps = lambda name, shape: st.enter_context(nc.psum_tensor(f"a2_{name}_{b}", shape, F32))
        q = [sb(f"q{r}", [P, TILE]) for r in range(2)]
        prob = [sb(f"prob{r}", [TILE, L]) for r in range(2)]
        probT = [sb(f"probT{r}", [TILE, 4, TILE]) for r in range(2)]
        o = [sb(f"o{r}", [TILE, P]) for r in range(2)]
        gmax = [sb(f"gmax{r}", [TILE, 4]) for r in range(2)]
        rmax = [sb(f"rmax{r}", [TILE, 1]) for r in range(2)]
        nmax = [sb(f"nmax{r}", [TILE, 1]) for r in range(2)]
        rsum = [sb(f"rsum{r}", [TILE, 1]) for r in range(2)]
        rinv = [sb(f"rinv{r}", [TILE, 1]) for r in range(2)]
        scp = [ps(f"scores{i}", [TILE, 2, 512]) for i in range(2)]
        tp = [ps(f"turned{i}", [TILE, 4, TILE]) for i in range(2)]
        op = ps("op", [TILE, P])
        otp = ps("otp", [P, TILE])
        q_ready, s_made, s_copied, max_step, max_ready, exp_done, turned, copied_v, copied_a, pv_done, inv_ready, o_normed, o_turned, o_placed = (
            sem(n) for n in ("q_ready", "s_made", "s_copied", "max_step", "max_ready", "exp_done", "turned", "copied_v", "copied_a", "pv_done", "inv_ready", "o_normed", "o_turned", "o_placed"))

        def copied(c, t):
            return (copied_v, 4 * (t + 1) + c // 2 + 1) if c % 2 == 0 else (copied_a, 3 * (t + 1) + c // 2 + 1)

        def copy_chunk(eng, copy, t, r, c, done):
            eng.wait_ge(turned, 7 * t + c + 1 + 14)
            if c >= 2:
                eng.wait_ge(pv_done, 7 * (t + 1) + c - 1)
            else:
                eng.wait_ge(pv_done, 7 * t + 6 + c)
            copy(probT[(r + c) % 2][:, :, :], tp[(r + c) % 2][:, :, :]).then_inc(done, 1)

        with nc.Block() as block:
            @block.gpsimd
            def _(pool):
                def stage_q(eng, t, r):
                    eng.wait_ge(s_made, 4 * (t + 1))
                    eng.tensor_copy(q[r][:, :], theta[:, bass.ds(TILE * t, TILE)]).then_inc(q_ready, 1)
                pipeline(pool, TILES, [(stage_q, 0)])

            @block.tensor
            def _(pe):
                def scores(eng, t, r):
                    eng.wait_ge(q_ready, t + 1)
                    for g in range(4):
                        eng.wait_ge(s_copied, 4 * t + g + 1)
                        for j in range(2):
                            at = SUB2 * (2 * g + j)
                            mm = eng.matmul(scp[g % 2][:, j, 0:SUB2], q[r][:, :], phi[:, at:at + SUB2], start=True, stop=True)
                        mm.then_inc(s_made, 1)

                def values(eng, t, r):
                    eng.wait_ge(exp_done, t + 1)
                    for c in range(CHUNKS + 1):
                        if c < CHUNKS:
                            eng.wait_ge(*(copied(c - 2, t) if c >= 2 else copied(c + 5, t - 1)))
                            for j in range(4):
                                at = TILE * (4 * c + j)
                                mm = eng.transpose(tp[(r + c) % 2][:, j, :], prob[r][:, at:at + TILE], m.ident[0:TILE, 0:TILE])
                            mm.then_inc(turned, 1)
                        if c == 1:
                            eng.wait_ge(o_normed, t + 1)
                        if c >= 1:
                            eng.wait_ge(*copied(c - 1, t))
                            for j in range(4):
                                k = 4 * (c - 1) + j
                                mm = eng.matmul(op[:, :], probT[(r + c - 1) % 2][:, j, :], gT[:, k, :], start=(k == 0), stop=(k == TILES - 1))
                            mm.then_inc(pv_done, 1)

                def turn_out(eng, t, r):
                    eng.wait_ge(o_normed, t + 2)
                    eng.wait_ge(o_placed, t + 1)
                    eng.transpose(otp[:, :], o[r][:, :], m.ident[0:TILE, 0:TILE]).then_inc(o_turned, 1)

                pe.sem_inc(s_made, 8)
                pe.sem_inc(turned, 14)
                pe.sem_inc(pv_done, 7)
                pe.sem_inc(o_turned, 2)
                pipeline(pe, TILES, [(scores, 0), (turn_out, 2), (values, 1)])

            @block.vector
            def _(dve):
                def row_max(eng, t, r):
                    eng.wait_ge(turned, 7 * (t + 1))
                    for g in range(4):
                        eng.wait_ge(s_made, 4 * t + g + 9)
                        eng.tensor_scalar(prob[r][:, 2 * SUB2 * g:2 * SUB2 * (g + 1)].rearrange("p (j c) -> p j c", j=2), scp[g % 2][:, :, 0:SUB2],
                                          1.0, None, ALU.mult, ALU.max, accum_out=gmax[r][:, g:g + 1]).then_inc(s_copied, 1)
                    eng.wait_ge(s_copied, 4 * t + 6)
                    eng.tensor_reduce(rmax[r][:, :], gmax[r][:, :], AX.X, ALU.max).then_inc(max_step, 1)
                    eng.wait_ge(max_step, t + 1)
                    eng.tensor_scalar(nmax[r][:, :], rmax[r][:, :], -1.0, None, ALU.mult).then_inc(max_ready, 1)

                def normalise(eng, t, r):
                    for c in (0, 2, 4, 6):
                        copy_chunk(eng, eng.tensor_copy, t, r, c, copied_v)
                    eng.reciprocal(rinv[r][:, :], rsum[r][:, :]).then_inc(inv_ready, 1)
                    eng.wait_ge(inv_ready, t + 1)
                    eng.wait_ge(pv_done, 7 * (t + 2))
                    eng.wait_ge(o_turned, t + 1)
                    eng.tensor_scalar(o[r][:, :], op[:, :], rinv[r][:, :], None, ALU.mult).then_inc(o_normed, 1)

                dve.sem_inc(s_copied, 2)
                dve.sem_inc(copied_v, 4)
                dve.sem_inc(o_normed, 1)
                pipeline(dve, TILES, [(row_max, 0), (normalise, 1)])

            @block.scalar
            def _(act):
                def copies(eng, t, r):
                    for c in (1, 3, 5):
                        copy_chunk(eng, eng.copy, t, r, c, copied_a)

                def place_out(eng, t, r):
                    eng.wait_ge(o_turned, t + 3)
                    eng.copy(nl[:, bass.ds(TILE * t, TILE)], otp[:, :]).then_inc(o_placed, 1)

                def exponent(eng, t, r):
                    eng.wait_ge(max_ready, t + 1)
                    eng.activation(prob[r][:, :], prob[r][:, :], ACT.Exp, bias=nmax[r][:, :], accum_out=rsum[r][:, :]).then_inc(exp_done, 1)

                act.sem_inc(copied_a, 3)
                act.sem_inc(o_placed, 1)
                pipeline(act, TILES, [(copies, 1), (place_out, 2), (exponent, 0)])
                act.wait_ge(o_placed, TILES + 1)


def project_out2(nc, m, b, s, nl):
    with ExitStack() as st:
        yp = [st.enter_context(nc.psum_tensor(f"y2p{i}_{b}", [P, 512], F32)) for i in range(8)]
        sem = st.enter_context(signals(nc, f"y2_{b}"))
        made, added, with_s = (sem(n) for n in ("made", "added", "with_s"))
        with nc.Block() as block:
            @block.tensor
            def _(pe):
                for n in range(HALVES * CHUNKS):
                    f, k = n // CHUNKS, n % CHUNKS
                    if n >= 8:
                        pe.wait_ge(added, n - 7)
                    pe.matmul(yp[n % 8][:, 0:CHUNK], m.WT[:, W_OUT + f, :], nl[:, CHUNK * k:CHUNK * (k + 1)], start=True, stop=True).then_inc(made, 1)

            @block.vector
            def _(dve):
                for f in range(HALVES):
                    X = m.X[:, HALVES * b + f, :]
                    dve.tensor_tensor(X, X, s[:, f, :], ALU.add).then_inc(with_s, 1)
                for n in range(HALVES * CHUNKS):
                    f, k = n // CHUNKS, n % CHUNKS
                    dve.wait_ge(made, n + 1)
                    dve.wait_ge(with_s, f + 1)
                    X = m.X[:, HALVES * b + f, CHUNK * k:CHUNK * (k + 1)]
                    dve.scalar_tensor_tensor(X, yp[n % 8][:, 0:CHUNK], m.bias2[:, 2 + f:3 + f], X, ALU.add, ALU.add).then_inc(added, 1)
                dve.wait_ge(added, HALVES * CHUNKS)


VPITCH = 3 * HD3


def attention3(nc, m):
    with ExitStack() as outer:
        keep = lambda name, shape: outer.enter_context(nc.sbuf_tensor(name, shape, F32))
        c = keep("spline_c", [P, 8])
        half_base = keep("half_base", [P, 1])
        linear = keep("linear", [P, 1])
        steps = [keep(f"diag_d{j + 1}", [P, P]) for j in range(2)]
        spline_constants3(nc, m, c, half_base, linear, steps)
        for b in range(B):
            with ExitStack() as st:
                buf = lambda name, shape: st.enter_context(nc.sbuf_tensor(f"{name}_{b}", shape, F32))
                Q, K = buf("Q3", [P, L]), buf("K3", [P, L])
                O = Q
                V = buf("V3", [TILE, TILES, 2 * VPITCH])
                project3(nc, m, b, Q, K, V)
                for pair in range(2):
                    kan_attention3(nc, m, b, pair, Q, K, V, O, c, half_base, linear, steps)
                project_out3(nc, m, b, O)


def spline_constants3(nc, m, c, half_base, linear, steps):
    with ExitStack() as st:
        prod = st.enter_context(nc.sbuf_tensor("sc_prod", [P, 8, 8], F32))
        scaled = st.enter_context(nc.sbuf_tensor("sc_scaled", [P, 8], F32))
        chain = st.enter_context(signals(nc, "sc"))("chain")
        with nc.Block() as block:
            @block.vector
            def _(dve):
                done = [0]

                def link(ins):
                    done[0] += 1
                    ins.then_inc(chain, 1)
                    dve.wait_ge(chain, done[0])
                link(dve.tensor_scalar(scaled[:, :], m.coef[:, :], m.scaler[:, :], None, ALU.mult))
                link(dve.tensor_tensor(prod[:, :, :], m.smat[:, :, :], scaled[:, :].unsqueeze(1).to_broadcast([P, 8, 8]), ALU.mult))
                link(dve.tensor_reduce(c[:, :], prod[:, :, :], AX.X, ALU.add))
                link(dve.tensor_scalar(half_base[:, :], m.basew[:, :], 0.5, None, ALU.mult))
                link(dve.tensor_tensor(linear[:, :], c[:, 2:3], half_base[:, :], ALU.add))
                for j in range(2):
                    link(dve.tensor_scalar(steps[j][:, :], m.ident[:, :], c[:, 5 + j:6 + j], None, ALU.mult))


def project3(nc, m, b, Q, K, V):
    scale = 1.0 / float(np.sqrt(HD3))
    with ExitStack() as st:
        xn = st.enter_context(nc.sbuf_tensor(f"xn3_{b}", [P, HALVES, L], F32))
        pp = [st.enter_context(nc.psum_tensor(f"p3p{i}_{b}", [P, 512], F32)) for i in range(8)]
        sem = st.enter_context(signals(nc, f"p3_{b}"))
        normed, made, kept_a, kept_v, ones_set = (sem(n) for n in ("normed", "made", "kept_a", "kept_v", "ones_set"))
        JOBS = 3 * CHUNKS
        with nc.Block() as block:
            @block.gpsimd
            def _(pool):
                pool.memset(V[:, :, 2 * HD3:VPITCH], 1.0).then_inc(ones_set, 1)
                pool.wait_ge(ones_set, 1)

            @block.vector
            def _(dve):
                for f in range(HALVES):
                    u = HALVES * b + f
                    dve.tensor_scalar(xn[:, f, :], m.X[:, u, :], m.rstd[:, u:u + 1], m.nbias[:, u:u + 1], ALU.mult, ALU.add).then_inc(normed, 1)
                for k in range(CHUNKS):
                    dve.wait_ge(made, 3 * k + 3)
                    for pair in range(2):
                        dve.tensor_copy(V[:, 4 * k:4 * k + 4, VPITCH * pair:VPITCH * pair + 2 * HD3],
                                        pp[(3 * k + 2) % 8][0:TILE, :].rearrange("p (j c) -> p j c", j=4)[:, :, 2 * HD3 * pair:2 * HD3 * (pair + 1)]).then_inc(kept_v, 1)
                dve.wait_ge(kept_v, 2 * CHUNKS)

            @block.scalar
            def _(act):
                for k in range(CHUNKS):
                    for j, dst in enumerate((Q, K)):
                        act.wait_ge(made, 3 * k + j + 1)
                        act.activation(dst[:, CHUNK * k:CHUNK * (k + 1)], pp[(3 * k + j) % 8][:, 0:CHUNK], ACT.Copy, scale=(scale, 1.0)[j]).then_inc(kept_a, 1)
                act.wait_ge(kept_a, 2 * CHUNKS)

            @block.tensor
            def _(pe):
                pe.wait_ge(normed, HALVES)
                for n in range(JOBS):
                    k, j = n // 3, n % 3
                    if n >= 8:
                        kk, jj = (n - 8) // 3, (n - 8) % 3
                        if jj == 2:
                            pe.wait_ge(kept_v, 2 * (kk + 1))
                        else:
                            pe.wait_ge(kept_a, 2 * kk + jj + 1)
                    bank = pp[n % 8]
                    if j < 2:
                        for i in range(HALVES):
                            mm = pe.matmul(bank[:, 0:CHUNK], m.WT[:, (W_Q3, W_K3)[j] + i, :], xn[:, i, CHUNK * k:CHUNK * (k + 1)],
                                           start=(i == 0), stop=(i == 1))
                    else:
                        for q in range(4):
                            at = TILE * (4 * k + q)
                            for i in range(HALVES):
                                mm = pe.matmul(bank[0:TILE, P * q:P * (q + 1)], xn[:, i, at:at + TILE], m.WT[:, W_V3 + i, :],
                                               start=(i == 0), stop=(i == 1))
                    mm.then_inc(made, 1)


def kan_attention3(nc, m, b, pair, Q, K, V, O, c, half_base, linear, steps):
    QUART = L // 4
    rows = slice(2 * HD3 * pair, 2 * HD3 * (pair + 1))
    with ExitStack() as st:
        tag = f"{b}{pair}"
        sem = st.enter_context(signals(nc, "a3_" + tag))
        sb = lambda name, shape: st.enter_context(nc.sbuf_tensor(f"a3_{name}_{tag}", shape, F32))
        ps = lambda name, shape: st.enter_context(nc.psum_tensor(f"a3_{name}_{tag}", shape, F32))
        q = [sb(f"q{r}", [P, P]) for r in range(2)]
        prob = [sb(f"prob{r}", [P, L]) for r in range(2)]
        probT = [sb(f"probT{r}", [TILE, 4, P]) for r in range(2)]
        x = [sb(f"x{g}", [P, QUART]) for g in range(4)]
        th = [sb(f"th{g}", [P, QUART]) for g in range(2)]
        v1 = [sb(f"v1{g}", [P, QUART]) for g in range(2)]
        v2 = [sb(f"v2{g}", [P, QUART]) for g in range(2)]
        s1 = [sb(f"s1{g}", [P, QUART]) for g in range(2)]
        s2 = [sb(f"s2{g}", [P, QUART]) for g in range(2)]
        right = sb("right", [P, QUART])
        knots = sb("knots", [P, 2])
        o = [sb(f"o{r}", [VPITCH, QT3]) for r in range(2)]
        gmax = [sb(f"gmax{r}", [P, 4]) for r in range(2)]
        rmax = [sb(f"rmax{r}", [P, 1]) for r in range(2)]
        nmax = [sb(f"nmax{r}", [P, 1]) for r in range(2)]
        rinv = [sb(f"rinv{r}", [VPITCH, QT3]) for r in range(2)]
        scp = ps("scores", [P, 2, 512])
        rp = ps("right_sides", [P, 2, 512])
        tp = [ps(f"turned{i}", [TILE, 4, P]) for i in range(2)]
        op = [ps(f"op{r}", [VPITCH, 512]) for r in range(2)]
        vcols = slice(2 * HD3 * pair, 2 * HD3 * pair + VPITCH)
        vrow, ones_rows = (0, slice(2 * HD3, VPITCH)) if pair == 0 else (HD3, slice(0, HD3))
        (q_ready, q_zeroed, knots_set, s_made, clipped, tanh_ready, v_ready, s_ready, cubed, right_made, right_gated,
         linear_made, inner_ready, tanh_added, based, left_added, all_added, max_step, max_ready, exp_done, turned, copied, pv_done,
         inv_ready, o_normed, o_placed, waits_met_v, waits_met_p) = (
            sem(n) for n in ("q_ready", "q_zeroed", "knots_set", "s_made", "clipped", "tanh_ready", "v_ready", "s_ready", "cubed",
                             "right_made", "right_gated", "linear_made", "inner_ready", "tanh_added", "based", "left_added", "all_added",
                             "max_step", "max_ready", "exp_done", "turned", "copied", "pv_done", "inv_ready", "o_normed",
                             "o_placed", "waits_met_v", "waits_met_p"))

        with nc.Block() as block:
            @block.gpsimd
            def _(pool):
                def stage_q(eng, t, r):
                    eng.wait_ge(s_made, 4 * (t + 1))
                    eng.wait_ge(cubed, 8 * t + 2)
                    for h in range(2):
                        hrows = slice(HD3 * (2 * pair + h), HD3 * (2 * pair + h + 1))
                        if h:
                            eng.wait_ge(q_ready, 2 * t + 1)
                        eng.tensor_copy(q[r][hrows, QT3 * h:QT3 * (h + 1)], Q[hrows, bass.ds(QT3 * t, QT3)]).then_inc(q_ready, 1)
                    eng.wait_ge(q_ready, 2 * t + 2)

                def inner(g):
                    def stage(eng, t, r):
                        f = prob[r][:, QUART * g:QUART * (g + 1)]
                        eng.wait_ge(turned, 7 * t + min(2 * g + 2, 7))
                        eng.wait_ge(clipped, 4 * t + g + 3)
                        eng.sem_inc(waits_met_p, 1)
                        eng.tensor_scalar(f, x[g][:, :], c[:, 0:1], c[:, 1:2], ALU.mult, ALU.add).then_inc(linear_made, 1)
                        eng.wait_ge(linear_made, 4 * t + g + 1)
                        eng.tensor_tensor(f, f, x[g][:, :], ALU.mult).then_inc(inner_ready, 1)
                    return stage

                def cubes(g):
                    def stage(eng, t, r):
                        n, G = 4 * t + g, g % 2
                        eng.wait_ge(s_ready, 2 * n + 1)
                        eng.tensor_tensor(v1[G][:, :], v1[G][:, :], s1[G][:, :], ALU.mult).then_inc(cubed, 1)
                        eng.wait_ge(s_ready, 2 * n + 2)
                        eng.tensor_tensor(v2[G][:, :], v2[G][:, :], s2[G][:, :], ALU.mult).then_inc(cubed, 1)
                    return stage

                for r in range(2):
                    pool.memset(q[r][rows, :], 0.0).then_inc(q_zeroed, 1)
                pool.wait_ge(q_zeroed, 2)
                for j, t in enumerate((KNOT_IN, KNOT_OUT)):
                    pool.memset(knots[:, j:j + 1], -t).then_inc(knots_set, 1)
                    pool.wait_ge(knots_set, j + 1)
                pool.sem_inc(cubed, 8)
                pipeline(pool, TILES3, [(stage_q, 0), (inner(1), 1), (cubes(1), 1), (inner(2), 1), (cubes(2), 1),
                                        (inner(3), 1), (cubes(3), 1), (inner(0), 0), (cubes(0), 0)])

            @block.tensor
            def _(pe):
                def scores(g):
                    def stage(eng, t, r):
                        if g == 0:
                            eng.wait_ge(q_ready, 2 * (t + 1))
                        eng.wait_ge(clipped, 4 * t + g + 2)
                        for j in range(2):
                            at = SUB * (2 * g + j)
                            mm = eng.matmul(scp[:, j, 0:SUB], q[r][rows, :], K[rows, at:at + SUB], start=True, stop=True)
                        mm.then_inc(s_made, 1)
                    return stage

                def right_side(g):
                    def stage(eng, t, r):
                        n, G = 4 * t + g, g % 2
                        eng.wait_ge(cubed, 2 * n + 10)
                        eng.wait_ge(right_gated, n + 1)
                        for j in range(2):
                            for i, v in enumerate((v1, v2)):
                                mm = eng.matmul(rp[:, j, 0:SUB], steps[i][:, :], v[G][:, SUB * j:SUB * (j + 1)], start=(i == 0), stop=(i == 1))
                        mm.then_inc(right_made, 1)
                    return stage

                def turn(ch):
                    def stage(eng, t, r):
                        if ch == 0:
                            eng.wait_ge(exp_done, 2 * t + 1)
                        if ch == 3:
                            eng.wait_ge(exp_done, 2 * t + 2)
                        eng.wait_ge(copied, 7 * t + ch + 1)
                        for j in range(4):
                            at = TILE * (4 * ch + j)
                            mm = eng.transpose(tp[(r + ch) % 2][:, j, :], prob[r][:, at:at + TILE], m.ident[:, :])
                        mm.then_inc(turned, 1)
                    return stage

                def weigh(ch):
                    def stage(eng, t, r):
                        if ch == 0:
                            eng.wait_ge(o_normed, 2 * (t + 1))
                        eng.wait_ge(copied, 7 * t + ch + 3)
                        for j in range(4):
                            k = 4 * ch + j
                            mm = eng.matmul(op[r][:, 0:P], V[:, k, vcols], probT[(r + ch) % 2][:, j, :], start=(k == 0), stop=(k == TILES - 1))
                        mm.then_inc(pv_done, 1)
                    return stage

                pe.sem_inc(s_made, 8)
                pe.sem_inc(turned, 14)
                pe.sem_inc(pv_done, 7)
                pe.sem_inc(right_made, 2)
                pipeline(pe, TILES3, [(turn(6), 3), (right_side(1), 1), (scores(0), 0), (weigh(6), 3),
                                      (turn(0), 2), (turn(1), 2), (right_side(2), 1), (weigh(0), 2), (scores(1), 0), (weigh(1), 2),
                                      (turn(2), 2), (turn(3), 2), (right_side(3), 1), (weigh(2), 2), (scores(2), 0), (weigh(3), 2),
                                      (turn(4), 2), (turn(5), 2), (right_side(0), 0), (weigh(4), 2), (scores(3), 0), (weigh(5), 2)])

            @block.vector
            def _(dve):
                def clip(g):
                    def stage(eng, t, r):
                        eng.wait_ge(s_made, 4 * t + g + 9)
                        eng.tensor_scalar(x[g][:, :].rearrange("p (j c) -> p j c", j=2), scp[:, :, 0:SUB], 6.0, -6.0, ALU.min, ALU.max).then_inc(clipped, 1)
                    return stage

                def base(g, part):
                    def stage(eng, t, r):
                        n, X, f = 4 * t + g, x[g][:, :], prob[r][:, QUART * g:QUART * (g + 1)]
                        if part == 0:
                            eng.wait_ge(tanh_ready, n + 1)
                            eng.wait_ge(inner_ready, n + 1)
                            eng.scalar_tensor_tensor(f, th[g % 2][:, :], half_base[:, :], f, ALU.mult, ALU.add).then_inc(tanh_added, 1)
                        else:
                            eng.wait_ge(tanh_added, n + 1)
                            eng.scalar_tensor_tensor(f, f, linear[:, :], X, ALU.add, ALU.mult).then_inc(based, 1)
                    return stage

                def left(g, part):
                    def stage(eng, t, r):
                        n, f = 4 * t + g, prob[r][:, QUART * g:QUART * (g + 1)]
                        eng.wait_ge(cubed, 2 * n + part + 9)
                        if part == 0:
                            eng.wait_ge(based, n + 3)
                        else:
                            eng.wait_ge(left_added, 2 * n + 5)
                        v = (v1, v2)[part][g % 2]
                        eng.scalar_tensor_tensor(f, v[:, :], c[:, 3 + part:4 + part], f, ALU.mult, ALU.add).then_inc(left_added, 1)
                    return stage

                def gate(g):
                    def stage(eng, t, r):
                        by_bank = lambda buf: buf[:, :].rearrange("p (j c) -> p j c", j=2)
                        eng.wait_ge(right_made, 4 * t + g + 3)
                        eng.wait_ge(all_added, 4 * t + g + 1)
                        eng.scalar_tensor_tensor(by_bank(right), by_bank(x[g]), 0.0, rp[:, :, 0:SUB], ALU.is_gt, ALU.mult).then_inc(right_gated, 1)
                    return stage

                def add_right(g):
                    def stage(eng, t, r):
                        n, f = 4 * t + g, prob[r][:, QUART * g:QUART * (g + 1)]
                        eng.wait_ge(right_gated, n + 2)
                        eng.wait_ge(left_added, 2 * n + 6)
                        eng.sem_inc(waits_met_v, 1)
                        eng.tensor_tensor_reduce(out=f, in0=f, in1=right[:, :], scale=1.0, scalar=-3.0e38, op0=ALU.add, op1=ALU.max,
                                                 accum_out=gmax[r][:, g:g + 1]).then_inc(all_added, 1)
                    return stage

                def row_max(eng, t, r):
                    eng.wait_ge(all_added, 4 * t + 5)
                    eng.tensor_reduce(rmax[r][:, :], gmax[r][:, :], AX.X, ALU.max).then_inc(max_step, 1)
                    eng.wait_ge(max_step, t + 1)
                    eng.tensor_scalar(nmax[r][:, :], rmax[r][:, :], -1.0, None, ALU.mult).then_inc(max_ready, 1)

                def normalise(eng, t, r):
                    vrows = [slice(vrow + HD3 * h, vrow + HD3 * (h + 1)) for h in range(2)]
                    eng.wait_ge(pv_done, 7 * (t + 2))
                    for h in range(2):
                        eng.reciprocal(rinv[r][vrows[h], :], op[r][ones_rows, QT3 * h:QT3 * (h + 1)]).then_inc(inv_ready, 1)
                    eng.wait_ge(o_placed, 2 * (t + 1))
                    for h in range(2):
                        eng.wait_ge(inv_ready, 2 * t + h + 1)
                        eng.tensor_tensor(o[r][vrows[h], :], op[r][vrows[h], QT3 * h:QT3 * (h + 1)], rinv[r][vrows[h], :], ALU.mult).then_inc(o_normed, 1)

                dve.sem_inc(clipped, 2)
                dve.sem_inc(based, 2)
                dve.sem_inc(left_added, 4)
                dve.sem_inc(right_gated, 1)
                dve.sem_inc(all_added, 1)
                dve.sem_inc(o_normed, 4)
                order = []
                for g in range(4):
                    b1, b2, b3 = ((g - back) % 4 for back in (1, 2, 3))
                    l1, l2, l3 = (int(g < back) for back in (1, 2, 3))
                    order.append((base(b2, 1), l2))
                    if g == 3:
                        order.append((row_max, 1))
                    order += [(gate(b3), l3), (left(b2, 0), l2), (clip(g), 0), (left(b2, 1), l2),
                              (base(b1, 0), l1), (add_right(b3), l3)]
                    if g == 0:
                        order.append((normalise, 3))
                pipeline(dve, TILES3, order)

            @block.scalar
            def _(act):
                def plane(g, which):
                    def stage(eng, t, r):
                        n, G = 4 * t + g, g % 2
                        if which == "tanh":
                            eng.wait_ge(clipped, n + 3)
                            eng.wait_ge(based, n + 1)
                            eng.activation(th[G][:, :], x[g][:, :], ACT.Tanh, scale=0.5).then_inc(tanh_ready, 1)
                        elif which == "abs":
                            eng.wait_ge(left_added, 2 * n + 2)
                            eng.wait_ge(right_made, n + 1)
                            eng.activation(v2[G][:, :], x[g][:, :], ACT.Abs).then_inc(v_ready, 1)
                        elif which == "v1":
                            eng.wait_ge(v_ready, 3 * n + 1)
                            eng.activation(v1[G][:, :], v2[G][:, :], ACT.Relu, bias=knots[:, 0:1]).then_inc(v_ready, 1)
                        elif which == "v2":
                            eng.wait_ge(v_ready, 3 * n + 2)
                            eng.activation(v2[G][:, :], v2[G][:, :], ACT.Relu, bias=knots[:, 1:2]).then_inc(v_ready, 1)
                        elif which == "s1":
                            eng.wait_ge(v_ready, 3 * n + 2)
                            eng.activation(s1[G][:, :], v1[G][:, :], ACT.Square).then_inc(s_ready, 1)
                        else:
                            eng.wait_ge(v_ready, 3 * n + 3)
                            eng.activation(s2[G][:, :], v2[G][:, :], ACT.Square).then_inc(s_ready, 1)
                    return stage

                def copies(ch):
                    def stage(eng, t, r):
                        eng.wait_ge(turned, 7 * t + ch + 15)
                        eng.wait_ge(pv_done, 7 * (t + 1) + ch - 1)
                        eng.copy(probT[(r + ch) % 2][:, :, :], tp[(r + ch) % 2][:, :, :]).then_inc(copied, 1)
                    return stage

                def place_out(eng, t, r):
                    eng.wait_ge(o_normed, 2 * (t + 3))
                    for h in range(2):
                        hrows = slice(HD3 * (2 * pair + h), HD3 * (2 * pair + h + 1))
                        eng.copy(O[hrows, bass.ds(QT3 * t, QT3)], o[r][vrow + HD3 * h:vrow + HD3 * (h + 1), :]).then_inc(o_placed, 1)

                def exponent(half):
                    def stage(eng, t, r):
                        half_row = prob[r][:, HALF * half:HALF * (half + 1)]
                        eng.wait_ge(max_ready, t + 1)
                        eng.activation(half_row, half_row, ACT.Exp, bias=nmax[r][:, :]).then_inc(exp_done, 1)
                    return stage

                act.wait_ge(knots_set, 2)
                act.sem_inc(copied, 2)
                act.sem_inc(o_placed, 4)
                planes = ("tanh", "abs", "v1", "s1", "v2", "s2")
                order = []
                for g, lag, chunks in ((0, 2, (0, 1)), (1, 2, (2, 3)), (2, 2, (4, 5)), (3, 2, (6,))):
                    order.append((plane(g, planes[0]), 0))
                    order += [(copies(ch), lag) for ch in chunks]
                    if g == 3:
                        order.append((exponent(0), 1))
                    if g == 0:
                        order.append((exponent(1), 2))
                    order += [(plane(g, w), 0) for w in planes[1:]]
                    if g == 1:
                        order.append((place_out, 3))
                pipeline(act, TILES3, order)
                act.wait_ge(o_placed, 2 * (TILES3 + 2))


def project_out3(nc, m, b, O):
    with ExitStack() as st:
        yp = [st.enter_context(nc.psum_tensor(f"y3p{i}_{b}", [P, 512], F32)) for i in range(8)]
        sem = st.enter_context(signals(nc, f"y3_{b}"))
        made, added = (sem(n) for n in ("made", "added"))
        with nc.Block() as block:
            @block.tensor
            def _(pe):
                for n in range(HALVES * CHUNKS):
                    f, k = n // CHUNKS, n % CHUNKS
                    if n >= 8:
                        pe.wait_ge(added, n - 7)
                    pe.matmul(yp[n % 8][:, 0:CHUNK], m.WT[:, W_O3 + f, :], O[:, CHUNK * k:CHUNK * (k + 1)], start=True, stop=True).then_inc(made, 1)

            @block.vector
            def _(dve):
                for n in range(HALVES * CHUNKS):
                    f, k = n // CHUNKS, n % CHUNKS
                    dve.wait_ge(made, n + 1)
                    X = m.X[:, HALVES * b + f, CHUNK * k:CHUNK * (k + 1)]
                    dve.tensor_tensor(X, X, yp[n % 8][:, 0:CHUNK], ALU.add).then_inc(added, 1)
                dve.wait_ge(added, HALVES * CHUNKS)


_INS = ["x", "L0_conv_qkv_w", "L0_conv_qkv_b", "L0_conv_proj_w", "L0_conv_proj_b", "L0_conv_relative_bias", "L1_conv_kernel",
        "L2_conv_cfc", "L2_conv_theta_w", "L2_conv_theta_b", "L2_conv_phi_w", "L2_conv_phi_b", "L2_conv_g_w", "L2_conv_g_b",
        "L2_conv_out_w", "L2_conv_out_b", "L3_conv_Wq", "L3_conv_Wk", "L3_conv_Wv", "L3_conv_Wo", "L3_conv_base_w",
        "L3_conv_spline_w", "L3_conv_spline_scaler"]


def kernel(**inputs):
    import numpy as _np
    import concourse.bacc as _bacc
    from concourse import mybir as _mybir
    from concourse.bass_utils import run_bass_kernel_spmd as _run

    nc = _bacc.Bacc("TRN2", target_bir_lowering=False, num_devices=1)
    arrays, args = {}, []
    values = [(name, inputs[name]) for name in _INS] + [("window_mask", window_mask()), ("spline_matrix", spline_matrix())]
    for name, value in values:
        a = _np.ascontiguousarray(value)
        arrays[f"in_{name}_dram"] = a
        args.append(nc.dram_tensor(f"in_{name}_dram", a.shape, _mybir.dt.from_np(a.dtype), kind="ExternalInput").ap())
    args.append(nc.dram_tensor("out_0_dram", (B, HALVES * P, IMG, IMG), F32, kind="ExternalOutput").ap())
    conv_preact_kernel(nc, *args)
    r = _run(nc, [arrays], core_ids=[0])
    return r.results[0]["out_0_dram"]
```
